# Optimizing a Trainium2 kernel written in Bass

```python
import numpy as np
import jax
import jax.numpy as jnp

def _softmax(x, axis=-1):
    return jax.nn.softmax(x, axis=axis)

def _gelu(x):
    return jax.nn.gelu(x, approximate=True)

def _silu(x):
    return jax.nn.silu(x)

def _sigmoid(x):
    return jax.nn.sigmoid(x)

def _layernorm(x, axis=-1, eps=1e-05):
    m = jnp.mean(x, axis=axis, keepdims=True)
    v = jnp.var(x, axis=axis, keepdims=True)
    return (x - m) / jnp.sqrt(v + eps)

def _scatter_add(tgt, idx, src, axis=0):
    return tgt.at[idx].add(src)

def _segment_sum(src, seg, n):
    return jax.ops.segment_sum(src, seg, n)
kernel_name = 'mk_macaron_d1_jaxref_r8_3cca5e'

def setup_inputs(seed: int=0):
    np.random.seed(seed)
    _w = jnp.asarray

    def _L0_attn_setup():
        import jax, jax.numpy as jnp
        import numpy as np
        N_HEAD = 16
        D_K = 64
        D_V = 64
        EMBED = 128
        BATCH = 4
        SEQ = 256
        key = jax.random.key(seed)
        ks = jax.random.split(key, 12)
        s = lambda d: 1.0 / np.sqrt(d)
        u = lambda k, shape, d: jax.random.uniform(k, shape, jnp.float32, -s(d), s(d))
        return {'z': jax.random.normal(ks[0], (BATCH, SEQ, EMBED), jnp.float32), 'wq': u(ks[1], (EMBED, D_K), D_K), 'wk': u(ks[2], (EMBED, D_K), D_K), 'wv': u(ks[3], (EMBED, D_V), D_V), 'fcq_w': u(ks[4], (D_K, N_HEAD * D_K), D_K), 'fcq_b': u(ks[5], (N_HEAD * D_K,), N_HEAD * D_K), 'fck_w': u(ks[6], (D_K, N_HEAD * D_K), D_K), 'fck_b': u(ks[7], (N_HEAD * D_K,), N_HEAD * D_K), 'fcv_w': u(ks[8], (D_V, N_HEAD * D_V), D_V), 'fcv_b': u(ks[9], (N_HEAD * D_V,), N_HEAD * D_V), 'fco_w': u(ks[10], (N_HEAD * D_V, EMBED), EMBED), 'fco_b': u(ks[11], (EMBED,), EMBED)}
    _L0_attn_in = _L0_attn_setup()

    def _L0_ffn_setup():
        import jax, jax.numpy as jnp
        import numpy as np
        DIM = 128
        HIDDEN = 384
        SCALE = 1.0 / 127.0

        def _dequant(w_int, dtype):
            return w_int.astype(dtype) * jnp.asarray(SCALE, dtype)
        key = jax.random.key(seed)
        k_x, k_g, k_u, k_d = jax.random.split(key, 4)
        x = jax.random.normal(k_x, (4, 256, DIM), dtype=jnp.float32)
        w_gate = jax.random.randint(k_g, (HIDDEN, DIM), -127, 128, dtype=jnp.int32)
        w_up = jax.random.randint(k_u, (HIDDEN, DIM), -127, 128, dtype=jnp.int32)
        w_down = jax.random.randint(k_d, (DIM, HIDDEN), -127, 128, dtype=jnp.int32)
        return {'x': x, 'w_gate': w_gate, 'w_up': w_up, 'w_down': w_down}
    _L0_ffn_in = _L0_ffn_setup()
    _d = {'L0_attn_z': _L0_attn_in['z'], 'L0_attn_wq': _L0_attn_in['wq'], 'L0_attn_wk': _L0_attn_in['wk'], 'L0_attn_wv': _L0_attn_in['wv'], 'L0_attn_fcq_w': _L0_attn_in['fcq_w'], 'L0_attn_fcq_b': _L0_attn_in['fcq_b'], 'L0_attn_fck_w': _L0_attn_in['fck_w'], 'L0_attn_fck_b': _L0_attn_in['fck_b'], 'L0_attn_fcv_w': _L0_attn_in['fcv_w'], 'L0_attn_fcv_b': _L0_attn_in['fcv_b'], 'L0_attn_fco_w': _L0_attn_in['fco_w'], 'L0_attn_fco_b': _L0_attn_in['fco_b'], 'L0_ffn_w_gate': _L0_ffn_in['w_gate'], 'L0_ffn_w_up': _L0_ffn_in['w_up'], 'L0_ffn_w_down': _L0_ffn_in['w_down']}
    _x0 = _d['L0_attn_z']
    _d['L0_attn_z'] = jax.random.normal(jax.random.fold_in(jax.random.key(seed), 1), (1, 2048, 128), dtype=_x0.dtype)
    del _x0
    return _d

def reference(L0_attn_z, L0_attn_wq, L0_attn_wk, L0_attn_wv, L0_attn_fcq_w, L0_attn_fcq_b, L0_attn_fck_w, L0_attn_fck_b, L0_attn_fcv_w, L0_attn_fcv_b, L0_attn_fco_w, L0_attn_fco_b, L0_ffn_w_gate, L0_ffn_w_up, L0_ffn_w_down):

    def _L0_attn_ref(z, wq, wk, wv, fcq_w, fcq_b, fck_w, fck_b, fcv_w, fcv_b, fco_w, fco_b):
        import jax, jax.numpy as jnp
        import numpy as np
        N_HEAD = 16
        D_K = 64
        D_V = 64
        EMBED = 128
        BATCH = 4
        SEQ = 256
        b, n, _ = z.shape
        scale = jnp.sqrt(jnp.float32(D_K))
        q = z @ wq @ fcq_w + fcq_b
        k = z @ wk @ fck_w + fck_b
        v = z @ wv @ fcv_w + fcv_b
        q = q.reshape(b, n, N_HEAD, D_K)
        k = k.reshape(b, n, N_HEAD, D_K)
        v = v.reshape(b, n, N_HEAD, D_V)
        scores = jnp.einsum('bihd,bjhd->bhij', q, k) / scale
        attn = jax.nn.softmax(scores, axis=-1)
        out = jnp.einsum('bhij,bjhd->bihd', attn, v)
        out = out.reshape(b, n, N_HEAD * D_V)
        return out @ fco_w + fco_b

    def _L0_ffn_ref(x, w_gate, w_up, w_down):
        import jax, jax.numpy as jnp
        import numpy as np
        DIM = 128
        HIDDEN = 384
        SCALE = 1.0 / 127.0

        def _dequant(w_int, dtype):
            return w_int.astype(dtype) * jnp.asarray(SCALE, dtype)
        wg = _dequant(w_gate, x.dtype)
        wu = _dequant(w_up, x.dtype)
        wd = _dequant(w_down, x.dtype)
        gate = jnp.einsum('bsd,hd->bsh', x, wg)
        up = jnp.einsum('bsd,hd->bsh', x, wu)
        h = jax.nn.silu(gate) * up
        return jnp.einsum('bsh,dh->bsd', h, wd)
    x = L0_attn_z
    x = x + 0.5 * _L0_ffn_ref(_layernorm(x, axis=-1), L0_ffn_w_gate, L0_ffn_w_up, L0_ffn_w_down)
    x = x + _L0_attn_ref(_layernorm(x, axis=-1), L0_attn_wq, L0_attn_wk, L0_attn_wv, L0_attn_fcq_w, L0_attn_fcq_b, L0_attn_fck_w, L0_attn_fck_b, L0_attn_fcv_w, L0_attn_fcv_b, L0_attn_fco_w, L0_attn_fco_b)
    x = x + 0.5 * _L0_ffn_ref(_layernorm(x, axis=-1), L0_ffn_w_gate, L0_ffn_w_up, L0_ffn_w_down)
    return x

_drawn_inputs = setup_inputs


def setup_inputs(seed=0):
    import zlib

    import numpy as np

    out = dict(_drawn_inputs(seed))
    spreads = {}
    factors = {'L0_attn_wq': 8.0,
     'L0_attn_wk': 8.0,
     'L0_attn_wv': 8.0,
     'L0_attn_fcq_w': 8.0,
     'L0_attn_fcq_b': 8.0,
     'L0_attn_fck_w': 8.0,
     'L0_attn_fck_b': 200.0,
     'L0_attn_fcv_w': 8.0,
     'L0_attn_fcv_b': 64.0,
     'L0_attn_fco_w': 8.0,
     'L0_attn_fco_b': 200.0}
    for name, (base, spread) in spreads.items():
        noise = np.random.default_rng([zlib.crc32(name.encode()), seed]).standard_normal(out[name].shape)
        drawn = base * np.exp(spread * noise) if base else spread * noise
        out[name] = jnp.asarray(drawn.astype(out[name].dtype))
    for name, factor in factors.items():
        out[name] = (out[name] * factor).astype(out[name].dtype)
    return out
```

```python
from contextlib import ExitStack

import concourse.bass as bass
from concourse import mybir

F32 = mybir.dt.float32
F32R = mybir.dt.float32r
F16 = mybir.dt.float16
I32 = mybir.dt.int32
ALU = mybir.AluOpType
ACT = mybir.ActivationFunctionType
AXX = mybir.AxisListType.X

P = 128
SEQ, EMBED, HIDDEN = 2048, 128, 384
HEADS, DK = 16, 64
EPS = 1e-5
SCALE = 1.0 / 127.0
T_RANGE = 4096.0

TILES = SEQ // P
QB = 512
NQB = SEQ // QB
TPB = QB // P
KPS = 2
SPB = TILES // KPS
HC = HIDDEN // P
G_ALL = HEADS * NQB
STEPS = G_ALL * SPB
AHEAD = 2
LAG = 3
PAIR = 2 * NQB * SPB
FIRST = 6
ROUNDS = HEADS // 2 - 1
RING = 4

FFN_ORDER = [("T", 0), ("T", 1), ("H", 0), ("T", 2), ("H", 1), ("D", 0), ("T", 3), ("H", 2), ("D", 1),
             ("H", 3), ("D", 2), ("D", 3)]


def side_jobs(t):
    g, j = divmod(t, SPB)
    h, b = divmod(g, NQB)
    jobs = []
    if j == 1 and g + 1 < G_ALL:
        jobs.append(("maxima", g + 1, 0))
    if j % 2 == 0 and h + 1 < HEADS and b < 2:
        jobs.append(("k" if b == 0 else "q", h + 1, j // 2))
    if j == 3 and g >= 1:
        jobs.append(("sums", g - 1, 0))
    if j == 5 and g >= 1:
        jobs.append(("out", g - 1, 0))
    return jobs


def has_scores(t):
    return t < STEPS


def has_product(t):
    return LAG <= t < STEPS + LAG


def has_maxima(t):
    return t < STEPS - AHEAD * SPB


SIDE_PER_PAIR = sum(len(side_jobs(PAIR + t)) for t in range(PAIR))
CHAIN_PER_PAIR = 2 * (NQB + NQB) + 2 * (2 * NQB)


class Turn:

    def __init__(self, local, turn, absolute):
        self.local = local
        self.turn = turn
        self.absolute = absolute

    def value(self, n, per_pair):
        return n if self.turn is None else self.turn * per_pair + n

    def t(self, offset=0):
        return self.value(self.local + offset, PAIR)


def run_steps(engine, step):
    for n in range(FIRST):
        step(Turn(n, None, n))
    with engine.Fori(0, ROUNDS) as turn:
        for n in range(FIRST, FIRST + PAIR):
            step(Turn(n, turn, n + PAIR))
    for n in range(ROUNDS * PAIR + FIRST, STEPS + SPB):
        step(Turn(n, None, n))


class Count:

    def __init__(self, per_pair):
        self.n = 0
        self.per_pair = per_pair
        self.entered = None

    def add(self, at):
        if at.turn is not None and self.entered is None:
            self.entered = self.n
        if at.turn is None and self.entered is not None:
            assert self.n == self.entered + self.per_pair, (self.n, self.entered, self.per_pair)
            self.n = self.entered + ROUNDS * self.per_pair
            self.entered = None
        self.n += 1

    def value(self, at, n=None):
        return at.value(self.n if n is None else n, self.per_pair)


def build(nc, z, wq, wk, wv, fcq_w, fcq_b, fck_w, fck_b, fcv_w, fcv_b, fco_w, fco_b, w_gate, w_up, w_down,
          out):
    ctx = ExitStack()
    with ctx:
        def sb(name, shape, dt=F32):
            return ctx.enter_context(nc.sbuf_tensor(name, shape, dt))

        def sem(name):
            return ctx.enter_context(nc.semaphore(name))

        X = sb("X", [P, TILES, EMBED])
        XN = sb("XN", [P, TILES, EMBED])
        XT = sb("XT", [P, SEQ])
        OUT = XN
        stats = sb("stats", [P, TILES, 6])
        meanvar = sb("meanvar", [P, TILES, 2])
        std = sb("std", [P, TILES])
        rstd = sb("rstd", [P, TILES])
        ident = sb("ident", [P, P])
        ones = sb("ones", [P, P])
        ones16 = sb("ones16", [P, 32], F16)
        quarter = sb("quarter", [P, 2])
        epsc = sb("epsc", [P, 1])
        w_int = sb("w_int", [P, 3, HIDDEN], I32)
        w_deq = sb("w_deq", [P, 3, HIDDEN])
        w_t = sb("w_t", [P, 3, HIDDEN])
        work = sb("work", [P, 2 * HC * QB])
        hT = work[:, :].rearrange("p (r c q) -> p r c q", r=2, c=HC)
        Pf = work[:, 0:2 * KPS * QB].rearrange("p (r n) -> p r n", r=2)
        sg = sb("sg", [P, 2, QB])
        w_in = sb("w_in", [P, 3, 2, DK])
        fqk = sb("fqk", [P, 2 * HEADS * DK])
        fq, fk = (fqk[:, i * HEADS * DK:(i + 1) * HEADS * DK].rearrange("p (h d) -> p h d", h=HEADS)
                  for i in range(2))
        Pl = fqk[:, :].bitcast(F16).rearrange("p (r n) -> p r n", r=RING)
        fv = sb("fv", [DK, HEADS * DK])
        fvT = sb("fvT", [P, HEADS // 2, 2, DK])
        fo_u = sb("fo_u", [P, HEADS // 2 * EMBED])
        fo = fo_u[:, :].rearrange("p (c e) -> p c e", e=EMBED)
        U, sums = fo_u[:, 0:QB], fo_u[:, QB:2 * QB]
        b_rows = sb("b_rows", [HEADS, 4, DK])
        bv_rows = sb("bv_rows", [HEADS // 2, P])
        bo_row = sb("bo_row", [1, EMBED])
        bqk = sb("bqk", [P, HEADS, 2])
        bh = sb("bh", [P, 2])
        bv = sb("bv", [P, HEADS // 2])
        W4 = sb("W4", [P, HEADS, 4, DK], F32R)
        Wh = sb("Wh", [P, 4, 2, DK], F32R)
        TQ = sb("TQ", [P, SEQ], F32R)
        TK = sb("TK", [P, SEQ], F32R)
        TV = sb("TV", [P, SEQ])
        TT = sb("TT", [P, TILES, 2, DK], F16)
        amax = sb("amax", [P, 1])
        asafe = sb("asafe", [P, 1])
        arec = sb("arec", [P, 1])
        ascale = sb("ascale", [P, 1])
        aback = sb("aback", [P, 1])
        GG = sb("GG", [P, HEADS * EMBED])
        bout = sb("bout", [P, EMBED])
        KK = [sb(f"KK{i}", [P, SEQ], F32R) for i in range(2)]
        K1 = [sb(f"K1{i}", [P, SEQ], F32R) for i in range(2)]
        QQ = [sb(f"QQ{i}", [P, SEQ], F32R) for i in range(2)]
        QL = [sb(f"QL{i}", [P, SEQ], F32R) for i in range(2)]
        pm = sb("pm", [P, 2, TPB, TILES // TPB])
        nmax = sb("nmax", [P, TPB])
        nm_parts = sb("nm_parts", [P, 2, TPB])
        nm_rows = sb("nm_rows", [2 * TPB, P])
        Ph = sb("Ph", [P, RING, KPS * QB], F16)
        rsum = sb("rsum", [P, TPB])

        banks = ctx.enter_context(nc.psum_tensor("banks", [P, 8, QB], F32))
        S = [banks[:, 0:2, :], banks[:, 2:4, :]]
        MB, SIDE, UB, SUMB = (banks[:, i, :] for i in range(4, 8))
        gate_banks = [banks[:, 0, :], banks[:, 1, :]]
        up_banks = [banks[:, 2, :], banks[:, 3, :]]
        gen_banks = [banks[:, i, :] for i in range(4, 8)]

        x_in = [sem(f"x_in{i}") for i in range(NQB)]
        wffn_in, watt_in, wfc_in = sem("wffn_in"), sem("watt_in"), sem("wfc_in")
        const_ready = sem("const_ready")
        dve_chain = sem("dve_chain")
        deq_ready = sem("deq_ready")
        stats_ready, std_ready, xn_ready = sem("stats_ready"), sem("std_ready"), sem("xn_ready")
        gen_full, gen_free = sem("gen_full"), sem("gen_free")
        gate_full, silu_ready = sem("gate_full"), sem("silu_ready")
        up_full, h_ready = sem("up_full"), sem("h_ready")
        tv_ready, bout_ready, x_biased = sem("tv_ready"), sem("bout_ready"), sem("x_biased")
        first_max_full, first_max_free = sem("first_max_full"), sem("first_max_free")
        scores_ready, exp_done, lo_ready, product_done = (
            sem("scores_ready"), sem("exp_done"), sem("lo_ready"), sem("product_done"))
        max_full, max_free = sem("max_full"), sem("max_free")
        side_full, side_free = sem("side_full"), sem("side_free")
        u_free = sem("u_free")
        nm_ready, nm_rows_ready, nm_written = sem("nm_ready"), sem("nm_rows_ready"), sem("nm_written")
        dve_loop = sem("dve_loop")
        weights_ready = sem("weights_ready")
        out_ready, stored = sem("out_ready"), sem("stored")

        W_FILLS = 5
        FFN_FILLS = 2 * NQB
        block = ctx.enter_context(nc.Block())

        def write_maxima_rows(sp, g, count):
            sp.wait_ge(nm_rows_ready, count)
            ql = QL[g // NQB % 2]
            b = g % NQB
            sp.dma_start(ql[DK:DK + 2, QB * b:QB * (b + 1)].bitcast(F32), nm_rows[:, :]).then_inc(nm_written, 16)

        def n_of(at, g):
            return g if at.turn is None else g - 2 * NQB

        def head_of(at, h):
            return h if at.turn is None else at.turn * 2 + (h - 2)

        def stage_weights(head):
            own = bass.ds(head, 1)
            for twice in range(2):
                nc.vector.tensor_copy(Wh[:, :, twice, :],
                                      W4[:, own, :, :].bitcast(F32).rearrange("p o a d -> p (o a) d"))
            return nc.vector.tensor_copy(bh[:, :], bqk[:, own, :].rearrange("p o a -> p (o a)"))

        def evacuate_k(h, b, full, link_):
            own = slice(QB * b, QB * (b + 1))
            kk, k1 = KK[h % 2], K1[h % 2]
            nc.vector.tensor_scalar(k1[0:DK, own], full[0:DK, :], bh[0:DK, 1:2], None, ALU.add)
            link_(nc.vector.tensor_scalar(kk[:, own], full, bh[:, 1:2], None, ALU.add))
            return nc.vector.scalar_tensor_tensor(kk[DK:P, own], full[DK:P, :], bh[DK:P, 1:2],
                                                  kk[DK:P, own].bitcast(F32), ALU.add, ALU.subtract)

        def evacuate_q(h, b, full, link_):
            own = slice(QB * b, QB * (b + 1))
            qq, ql = QQ[h % 2], QL[h % 2]
            link_(nc.vector.tensor_scalar(qq[:, own], full, bh[:, 0:1], None, ALU.add))
            return nc.vector.scalar_tensor_tensor(ql[0:DK, own], full[0:DK, :], bh[0:DK, 0:1],
                                                  qq[0:DK, own].bitcast(F32), ALU.add, ALU.subtract)

        def negate_maxima(g, link_):
            link_(nc.vector.tensor_reduce(nmax[:, :], pm[:, g % 2, :, :], AXX, ALU.max, negate=True))
            link_(nc.vector.tensor_copy(nm_parts[:, 0, :].bitcast(F32R), nmax[:, :]))
            return nc.vector.tensor_tensor(nm_parts[:, 1, :].bitcast(F32R), nmax[:, :], nm_parts[:, 0, :],
                                           ALU.subtract)

        @block.sync
        def _(sp):
            z_view = z.rearrange("o (b t p) d -> b p (o t) d", p=P, t=TPB)
            for b in range(NQB):
                sp.dma_start(X[:, TPB * b:TPB * (b + 1), :], z_view[b]).then_inc(x_in[b], 16)
            for i, w in enumerate((wq, wk, wv)):
                for twice in range(2):
                    sp.dma_start(w_in[:, i, twice, :], w).then_inc(watt_in, 16)
            sp.wait_ge(const_ready, 11)
            for g in range(1):
                write_maxima_rows(sp, g, g + 1)
            with sp.Fori(0, ROUNDS) as turn:
                for g in range(1, 1 + 2 * NQB):
                    write_maxima_rows(sp, g, turn * (2 * NQB) + (g + 1))
            for g in range(1 + ROUNDS * 2 * NQB, G_ALL):
                write_maxima_rows(sp, g, g + 1)
            out_view = out.rearrange("o (b t p) d -> b p (o t) d", p=P, t=TPB)
            for b in range(NQB):
                sp.wait_ge(out_ready, b + 1)
                sp.dma_start(out_view[b], OUT[:, TPB * b:TPB * (b + 1), :]).then_inc(stored, 16)
            sp.wait_ge(stored, 16 * NQB)

        @block.gpsimd
        def _(pool):
            def fill(ins, n):
                ins.then_inc(const_ready, 1)
                pool.wait_ge(const_ready, n)

            fill(nc.gpsimd.memset(ident[:, :], 0.0), 1)
            fill(nc.gpsimd.affine_select(out=ident[:, :], in_=ident[:, :], compare_op=ALU.not_equal, fill=1.0,
                                         base=0, pattern=[[-1, P]], channel_multiplier=1), 2)
            fill(nc.gpsimd.memset(ones[:, :], 1.0), 3)
            fill(nc.gpsimd.memset(ones16[:, :], 1.0), 4)
            fill(nc.gpsimd.memset(quarter[:, :], 1.0 / 32.0), 5)
            for i in range(2):
                fill(nc.gpsimd.memset(QL[i][DK:P, :].bitcast(F32), 0.0), 6 + 3 * i)
                fill(nc.gpsimd.memset(K1[i][DK:P, :].bitcast(F32), 0.0), 7 + 3 * i)
                fill(nc.gpsimd.memset(K1[i][DK:DK + 2, :].bitcast(F32), 1.0), 8 + 3 * i)
            pool.wait_ge(bout_ready, 1)
            pool.wait_ge(xn_ready, 2 * NQB)
            for t in range(TILES):
                nc.gpsimd.tensor_tensor(X[:, t, :], X[:, t, :], bout[:, :], ALU.add).then_inc(x_biased, 1)

            def step(at):
                t = at.absolute
                if not has_scores(t):
                    return
                pool.wait_ge(exp_done, at.t(1))
                if t >= RING:
                    pool.wait_ge(product_done, at.t(1 - RING))
                nc.gpsimd.tensor_tensor(Pl[:, t % RING, :], Pf[:, t % 2, :], Ph[:, t % RING, :],
                                        ALU.subtract).then_inc(lo_ready, 1)

            run_steps(nc.gpsimd, step)

        @block.scalar
        def _(act):
            for i, w in enumerate((w_gate, w_up)):
                act.dma_start(w_int[:, i, :].rearrange("p (c d) -> p c d", c=HC),
                              w.rearrange("(c p) d -> p c d", p=P)).then_inc(wffn_in, 16)
            act.dma_start(w_int[:, 2, :], w_down).then_inc(wffn_in, 16)
            for rows, w in ((b_rows[:, 0, :], fcq_b), (b_rows[:, 1, :], fcq_b),
                            (b_rows[:, 2, :], fck_b), (b_rows[:, 3, :], fck_b)):
                act.dma_start(rows, w.rearrange("(h d) -> h d", d=DK)).then_inc(wfc_in, 16)
            act.dma_start(bv_rows[:, :], fcv_b.rearrange("(h d) -> h d", d=P)).then_inc(wfc_in, 16)
            act.dma_start(bo_row[:, :], fco_b.rearrange("(o d) -> o d", o=1)).then_inc(wfc_in, 16)
            act.dma_start(fv[:, :], fcv_w).then_inc(wfc_in, 16)
            act.dma_start(fo[:, :, :], fco_w.rearrange("(c p) e -> p c e", p=P)).then_inc(wfc_in, 16)
            for f, w in ((fq, fcq_w), (fk, fck_w)):
                for half in range(2):
                    act.dma_start(f[DK * half:DK * (half + 1), :, :].rearrange("p h d -> p (h d)"),
                                  w).then_inc(wfc_in, 16)

            def layer_norm(n):
                act.wait_ge(stats_ready, n + 1)
                nc.scalar.activation(std[:, :], meanvar[:, :, 1], ACT.Sqrt, bias=epsc[:, :]).then_inc(std_ready, 1)

            def ffn(n):
                for b in range(NQB):
                    for c in range(HC):
                        k = (n * NQB + b) * HC + c
                        act.wait_ge(gate_full, k + 1)
                        if k >= 2:
                            act.wait_ge(h_ready, k - 1)
                        nc.scalar.activation(sg[:, k % 2, :], gate_banks[k % 2], ACT.Silu).then_inc(silu_ready, 1)

            layer_norm(0)
            ffn(0)
            layer_norm(1)

            def step(at):
                t = at.absolute
                if not has_scores(t):
                    return
                act.wait_ge(scores_ready, at.t(1))
                if t >= RING:
                    act.wait_ge(product_done, at.t(1 - RING))
                scores = S[t % 2]
                nc.scalar.activation(Ph[:, t % RING, :].rearrange("p (k q) -> p k q", k=KPS), scores, ACT.Exp)
                if t >= 2:
                    act.wait_ge(lo_ready, at.t(-1))
                nc.scalar.activation(Pf[:, t % 2, :].rearrange("p (k q) -> p k q", k=KPS), scores,
                                     ACT.Exp).then_inc(exp_done, 1)

            run_steps(nc.scalar, step)
            layer_norm(2)
            ffn(1)

        @block.vector
        def _(dve):
            chained = [0]
            gen = [0]

            def link(ins):
                chained[0] += 1
                ins.then_inc(dve_chain, 1)
                dve.wait_ge(dve_chain, chained[0])

            def take():
                gen[0] += 1
                dve.wait_ge(gen_full, gen[0])
                return gen_banks[(gen[0] - 1) % 4]

            def layer_norm(n):
                for t in range(TILES):
                    if n == 0 and t % TPB == 0:
                        dve.wait_ge(x_in[t // TPB], 16)
                    last = nc.vector.bn_stats(stats[:, t, :], X[:, t, :])
                link(last)
                for t in range(TILES):
                    last = nc.vector.bn_aggr(meanvar[:, t, :], stats[:, t, :])
                last.then_inc(stats_ready, 1)
                dve.wait_ge(stats_ready, n + 1)
                dve.wait_ge(std_ready, n + 1)
                link(nc.vector.reciprocal(rstd[:, :], std[:, :]))
                for t in range(TILES):
                    ins = nc.vector.tensor_scalar(XN[:, t, :], X[:, t, :], meanvar[:, t, 0:1], rstd[:, t:t + 1],
                                                  ALU.subtract, ALU.mult)
                    if t % TPB == TPB - 1:
                        ins.then_inc(xn_ready, 1)

            def ffn(n):
                for what, b in FFN_ORDER:
                    if what == "T":
                        nc.vector.tensor_copy(XT[:, QB * b:QB * (b + 1)], take()).then_inc(gen_free, 1)
                    elif what == "H":
                        for c in range(HC):
                            k = (n * NQB + b) * HC + c
                            dve.wait_ge(up_full, k + 1)
                            dve.wait_ge(silu_ready, k + 1)
                            nc.vector.tensor_tensor(hT[:, b % 2, c, :], up_banks[k % 2], sg[:, k % 2, :],
                                                    ALU.mult).then_inc(h_ready, 1)
                    else:
                        full = take().rearrange("p (t d) -> p t d", t=TPB)
                        own = slice(TPB * b, TPB * (b + 1))
                        ins = nc.vector.scalar_tensor_tensor((X if n == 0 else OUT)[:, own, :], full, 0.5,
                                                             X[:, own, :], ALU.mult, ALU.add)
                        ins.then_inc(gen_free, 1)
                        if n == 1:
                            dve.wait_ge(gen_free, gen[0])
                            nc.vector.tensor_copy(rsum[:, 0:1], epsc[:, :]).then_inc(out_ready, 1)

            nc.vector.memset(epsc[:, :], EPS).then_inc(dve_chain, 1)
            chained[0] += 1
            dve.wait_ge(wffn_in, 16 * 3)
            for i in range(3):
                nc.vector.tensor_scalar(w_deq[:, i, :], w_int[:, i, :], SCALE, None, ALU.mult).then_inc(deq_ready, 1)
            layer_norm(0)
            for i in range(3):
                nc.vector.tensor_copy(w_t[:, i, :], take()[:, 0:HIDDEN]).then_inc(gen_free, 1)
            full = take()
            nc.vector.tensor_scalar(bqk[:, :, 0], full[:, 0:HEADS], DK ** -0.5, None, ALU.mult)
            nc.vector.tensor_copy(bqk[:, :, 1], full[:, HEADS:2 * HEADS])
            nc.vector.tensor_copy(bv[:, :], full[:, 2 * HEADS:2 * HEADS + HEADS // 2]).then_inc(gen_free, 1)
            full = take().rearrange("p (c d) -> p c d", c=HEADS // 2)
            nc.vector.tensor_copy(fvT[:, :, 0, :], full)
            nc.vector.tensor_copy(fvT[:, :, 1, :], full).then_inc(gen_free, 1)
            ffn(0)
            dve.wait_ge(gen_free, gen[0])
            layer_norm(1)
            for i, (f, scale) in enumerate(((fq, DK ** -0.5), (fk, 1.0))):
                link(nc.vector.tensor_scalar(W4[:, :, 2 * i, :], f[:, :, :], scale, None, ALU.mult))
                link(nc.vector.scalar_tensor_tensor(W4[:, :, 2 * i + 1, :], f[:, :, :], scale,
                                                    W4[:, :, 2 * i, :].bitcast(F32), ALU.mult, ALU.subtract))
            for b in range(NQB):
                nc.vector.tensor_copy(XT[:, QB * b:QB * (b + 1)], take()).then_inc(gen_free, 1)
            link(stage_weights(0))
            for T in (TK, TQ):
                for b in range(NQB):
                    full, own = take(), slice(QB * b, QB * (b + 1))
                    link(nc.vector.tensor_copy(T[:, own], full))
                    nc.vector.tensor_tensor(T[DK:P, own], full[DK:P, :], T[DK:P, own].bitcast(F32),
                                            ALU.subtract).then_inc(gen_free, 1)
            for b in range(NQB):
                evacuate_k(0, b, take(), link).then_inc(gen_free, 1)
            for b in range(NQB):
                evacuate_q(0, b, take(), link).then_inc(gen_free, 1)
            for i in range(AHEAD * TPB * 2):
                tile, half = divmod(i, 2)
                g, tile = divmod(tile, TPB)
                dve.wait_ge(first_max_full, i + 1)
                nc.vector.reduce_max(pm[:, g, tile, 2 * half:2 * half + 2], S[i % 2], AXX).then_inc(first_max_free, 1)
            dve.wait_ge(first_max_free, AHEAD * TPB * 2)
            negate_maxima(0, link).then_inc(nm_ready, 1)
            nc.vector.tensor_copy(nm_rows[:, :], take()[0:2 * TPB, 0:P]).then_inc(nm_rows_ready, 1)
            dve.wait_ge(nm_rows_ready, 1)
            nc.vector.tensor_copy(rsum[:, 0:1], epsc[:, :]).then_inc(gen_free, 1)
            for b in range(NQB):
                ins = nc.vector.tensor_copy(TV[:, QB * b:QB * (b + 1)], take())
                ins.then_inc(gen_free, 1)
            dve.wait_ge(gen_free, gen[0])
            link(nc.vector.tensor_reduce(amax[:, :], TV[:, :], AXX, ALU.max, apply_absolute_value=True))
            link(nc.vector.tensor_scalar(asafe[:, :], amax[:, :], 1e-30, None, ALU.max))
            link(nc.vector.reciprocal(arec[:, :], asafe[:, :]))
            link(nc.vector.tensor_scalar(ascale[:, :], arec[:, :], T_RANGE, None, ALU.mult))
            link(nc.vector.tensor_scalar(aback[:, :], asafe[:, :], 1.0 / T_RANGE, None, ALU.mult))
            nc.vector.tensor_scalar(TV[:, :], TV[:, :], ascale[:, :], None, ALU.mult).then_inc(tv_ready, 1)
            half_tiles = TILES // 2
            for i in range(2):
                full = take().rearrange("p (t d) -> p t d", t=half_tiles)
                own = slice(half_tiles * i, half_tiles * (i + 1))
                link(nc.vector.tensor_copy(TT[:, own, 0, :], full))
                nc.vector.tensor_tensor(TT[:, own, 1, :], full, TT[:, own, 0, :], ALU.subtract).then_inc(gen_free, 1)
            for i in range(4):
                own = GG[:, :].rearrange("p (a k r e) -> p a k r e", a=2, k=4, r=2)[:, i // 2, :, i % 2, :]
                nc.vector.tensor_scalar(own, take().rearrange("p (k e) -> p k e", k=4), aback[:, :], None,
                                        ALU.mult).then_inc(gen_free, 1)
            nc.vector.tensor_copy(bout[:, :], take()[:, 0:EMBED]).then_inc(gen_free, 1)
            dve.wait_ge(gen_free, gen[0])
            nc.vector.tensor_copy(rsum[:, 0:1], epsc[:, :]).then_inc(bout_ready, 1)

            side = Count(SIDE_PER_PAIR)
            chain = Count(CHAIN_PER_PAIR)

            def step(at):
                t = at.absolute
                g, j = divmod(t, SPB)
                b = g % NQB

                def loop_link(ins):
                    chain.add(at)
                    ins.then_inc(dve_loop, 1)
                    dve.wait_ge(dve_loop, chain.value(at))

                if j == LAG and g >= 1 and g - 1 < G_ALL:
                    dve.wait_ge(product_done, at.t(-LAG))
                    nc.vector.tensor_copy(U[:, :], UB)
                    nc.vector.tensor_copy(sums[:, :], SUMB).then_inc(u_free, 1)
                if has_maxima(t):
                    for i in range(2):
                        dve.wait_ge(max_full, at.value(2 * at.local + i + 1, 2 * PAIR))
                        chunk = 2 * (j % 2) + i
                        nc.vector.reduce_max(pm[:, g % 2, j // 2, chunk:chunk + 1], MB, AXX).then_inc(max_free, 1)
                if j == 0 and g + 1 < G_ALL:
                    if g >= 1:
                        dve.wait_ge(max_free, at.value(2 * at.local, 2 * PAIR))
                    negate_maxima(g + 1, loop_link).then_inc(nm_ready, 1)
                for job, n, i in side_jobs(t):
                    side.add(at)
                    dve.wait_ge(side_full, side.value(at))
                    if job == "maxima":
                        dve.wait_ge(nm_written, at.value(16 * n_of(at, n), 16 * 2 * NQB))
                        nc.vector.tensor_copy(nm_rows[:, :], SIDE[0:2 * TPB, 0:P]).then_inc(nm_rows_ready, 1)
                        dve.wait_ge(nm_rows_ready, at.value(n_of(at, n) + 1, 2 * NQB))
                        nc.vector.tensor_copy(amax[:, :], epsc[:, :]).then_inc(side_free, 1)
                    elif job == "k":
                        evacuate_k(n, i, SIDE, loop_link).then_inc(side_free, 1)
                    elif job == "q":
                        evacuate_q(n, i, SIDE, loop_link).then_inc(side_free, 1)
                    elif job == "sums":
                        nc.vector.reciprocal(rsum[:, :], SIDE[:, 0:2 * TPB].rearrange("p (t o) -> p t o", o=2)[:, :, 0]
                                             ).then_inc(side_free, 1)
                    else:
                        dve.wait_ge(side_free, side.value(at, side.n - 1))
                        if g == 1:
                            dve.wait_ge(x_biased, TILES)
                        for q in range(TPB):
                            tile = TPB * (n % NQB) + q
                            ins = nc.vector.scalar_tensor_tensor(X[:, tile, :], SIDE[:, P * q:P * (q + 1)],
                                                                 rsum[:, q:q + 1], X[:, tile, :], ALU.mult, ALU.add)
                        ins.then_inc(side_free, 1)
                if b == 2 and j == SPB - 1 and g // NQB + 2 < HEADS:
                    stage_weights(head_of(at, g // NQB + 2)).then_inc(weights_ready, 1)

            stage_weights(1).then_inc(weights_ready, 1)
            run_steps(nc.vector, step)
            dve.wait_ge(side_free, side.n)
            layer_norm(2)
            ffn(1)

        @block.tensor
        def _(pe):
            gen = [0]

            def give():
                gen[0] += 1
                if gen[0] > 4:
                    pe.wait_ge(gen_free, gen[0] - 4)
                return gen_banks[(gen[0] - 1) % 4]

            def transpose(to, of):
                k, m = of.shape
                return nc.tensor.transpose(to, of, ident[0:k, 0:k])

            def block_transposes(n, b):
                full = give()
                pe.wait_ge(xn_ready, n * NQB + b + 1)
                for i in range(TPB):
                    last = transpose(full[:, P * i:P * (i + 1)], XN[:, TPB * b + i, :])
                last.then_inc(gen_full, 1)

            def ffn(n, emptied):
                blocks_emptied = {}
                done = emptied
                for what, b in FFN_ORDER:
                    if what == "T":
                        block_transposes(2 * n if n else 0, b)
                        done += 1
                        blocks_emptied[b] = done
                    elif what == "H":
                        pe.wait_ge(gen_free, blocks_emptied[b])
                        for c in range(HC):
                            k = (n * NQB + b) * HC + c
                            if k >= 2:
                                pe.wait_ge(h_ready, k - 1)
                            for full, w, done_sem in ((gate_banks, 0, gate_full), (up_banks, 1, up_full)):
                                nc.tensor.matmul(full[k % 2], w_t[:, w, P * c:P * (c + 1)],
                                                 XT[:, QB * b:QB * (b + 1)], start=True, stop=True
                                                 ).then_inc(done_sem, 1)
                    else:
                        full = give()
                        done += 1
                        pe.wait_ge(h_ready, (n * NQB + b + 1) * HC)
                        for i in range(TPB):
                            for c in range(HC):
                                last = nc.tensor.matmul(full[:, P * i:P * (i + 1)],
                                                        hT[:, b % 2, c, P * i:P * (i + 1)],
                                                        w_t[:, 2, P * c:P * (c + 1)], start=c == 0, stop=c == HC - 1)
                        last.then_inc(gen_full, 1)

            def project(full, parts, T, b):
                for i in range(2):
                    last = nc.tensor.matmul(full, Wh[:, parts + i, :, :].rearrange("p a d -> p (a d)"),
                                            T[:, QB * b:QB * (b + 1)], start=i == 0, stop=i == 1)
                return last

            pe.wait_ge(const_ready, 2)
            for i in range(3):
                full = give()
                pe.wait_ge(deq_ready, i + 1)
                for c in range(HC):
                    last = transpose(full[:, P * c:P * (c + 1)], w_deq[:, i, P * c:P * (c + 1)])
                last.then_inc(gen_full, 1)
            full = give()
            pe.wait_ge(wfc_in, 16 * 12)
            transpose(full[:, 0:HEADS], b_rows[:, 0:2, :].rearrange("p a d -> p (a d)"))
            transpose(full[:, HEADS:2 * HEADS], b_rows[:, 2:4, :].rearrange("p a d -> p (a d)"))
            transpose(full[:, 2 * HEADS:2 * HEADS + HEADS // 2], bv_rows[:, :]).then_inc(gen_full, 1)
            full = give()
            for c in range(HEADS // 2):
                last = transpose(full[:, DK * c:DK * (c + 1)], fv[:, P * c:P * (c + 1)])
            last.then_inc(gen_full, 1)
            pe.wait_ge(gen_free, 3)
            ffn(0, W_FILLS)
            for b in range(NQB):
                block_transposes(1, b)
            base = gen[0]
            pe.wait_ge(watt_in, 16 * 6)

            def input_projection(i):
                for b in range(NQB):
                    full = give()
                    pe.wait_ge(gen_free, base - NQB + b + 1)
                    nc.tensor.matmul(full, w_in[:, i, :, :].rearrange("p a d -> p (a d)"),
                                     XT[:, QB * b:QB * (b + 1)], start=True, stop=True).then_inc(gen_full, 1)

            input_projection(1)
            input_projection(0)
            for parts, T, before in ((2, TK, base + NQB), (0, TQ, base + 2 * NQB)):
                for b in range(NQB):
                    full = give()
                    pe.wait_ge(gen_free, before - NQB + NQB - (NQB - 1 - b))
                    project(full, parts, T, b).then_inc(gen_full, 1)
            pe.wait_ge(gen_free, gen[0])
            for i in range(AHEAD * TPB * 2):
                tile, half = divmod(i, 2)
                if i >= 2:
                    pe.wait_ge(first_max_free, i - 1)
                for c in range(2):
                    keys = QB * (2 * half + c)
                    last = nc.tensor.matmul(S[i % 2][:, c, :], QQ[0][:, P * tile:P * (tile + 1)],
                                            KK[0][:, keys:keys + QB], start=True, stop=True)
                last.then_inc(first_max_full, 1)
            full = give()
            pe.wait_ge(nm_ready, 1)
            transpose(full[0:2 * TPB, 0:P], nm_parts[:, :, :].rearrange("p a t -> p (a t)")).then_inc(gen_full, 1)
            input_projection(2)
            pe.wait_ge(tv_ready, 1)
            for i in range(2):
                full = give()
                for t in range(TILES // 2):
                    tile = TILES // 2 * i + t
                    last = transpose(full[:, DK * t:DK * (t + 1)], TV[0:DK, P * tile:P * (tile + 1)])
                last.then_inc(gen_full, 1)
            for i in range(4):
                full = give()
                for k in range(4):
                    h = 8 * (i // 2) + 2 * k + i % 2
                    rows = slice(DK * (h % 2), DK * (h % 2 + 1))
                    last = nc.tensor.matmul(full[:, P * k:P * (k + 1)],
                                            fvT[rows, h // 2, :, :].rearrange("p a d -> p (a d)"),
                                            fo[rows, h // 2, :], start=True, stop=True)
                last.then_inc(gen_full, 1)
            full = give()
            pe.wait_ge(const_ready, 11)
            for c in range(HEADS // 2):
                nc.tensor.matmul(full[:, 0:EMBED], bv[:, c:c + 1].to_broadcast([P, P]), fo[:, c, :],
                                 start=c == 0, stop=False)
            nc.tensor.matmul(full[:, 0:EMBED], ones[0:1, :], bo_row[:, :], start=False, stop=True
                             ).then_inc(gen_full, 1)
            pe.wait_ge(gen_free, gen[0])
            pe.wait_ge(first_max_free, AHEAD * TPB * 2)

            side = Count(SIDE_PER_PAIR)

            def maxima(at, i):
                t = at.absolute
                g, j = divmod(t, SPB)
                gm = g + AHEAD
                hm, bm = divmod(gm, NQB)
                tile = TPB * bm + j // 2
                keys = QB * (2 * (j % 2) + i)
                if t > 0 or i > 0:
                    pe.wait_ge(max_free, at.value(2 * at.local + i, 2 * PAIR))
                nc.tensor.matmul(MB, QQ[hm % 2][:, P * tile:P * (tile + 1)], KK[hm % 2][:, keys:keys + QB],
                                 start=True, stop=True).then_inc(max_full, 1)

            def step(at):
                t = at.absolute
                g, j = divmod(t, SPB)
                b, h = g % NQB, g // NQB
                if has_scores(t):
                    if j == 0:
                        pe.wait_ge(nm_written, at.value(16 * (n_of(at, g) + 1), 16 * 2 * NQB))
                    if t >= 2:
                        pe.wait_ge(exp_done, at.t(-1))
                    cols = slice(QB * b, QB * (b + 1))
                    for k in range(KPS):
                        tile = KPS * j + k
                        keys = slice(P * tile, P * (tile + 1))
                        nc.tensor.matmul(S[t % 2][:, k, :], KK[h % 2][:, keys], QQ[h % 2][:, cols],
                                         start=True, stop=False)
                        last = nc.tensor.matmul(S[t % 2][:, k, :], K1[h % 2][:, keys], QL[h % 2][:, cols],
                                                start=False, stop=True)
                    last.then_inc(scores_ready, 1)
                if has_maxima(t):
                    if b == 2 and j == 0:
                        pe.wait_ge(side_free, side.value(at))
                    maxima(at, 0)
                if has_product(t):
                    s = t - LAG
                    js = s % SPB
                    pe.wait_ge(lo_ready, at.t(1 - LAG))
                    if js == 0 and s >= SPB:
                        pe.wait_ge(u_free, at.value(n_of(at, s // SPB), 2 * NQB))
                    for k in range(KPS):
                        tile = KPS * js + k
                        nc.tensor.matmul(UB, TT[:, tile, :, :].rearrange("p a d -> p (a d)"),
                                         Ph[:, s % RING, QB * k:QB * (k + 1)], start=js == 0 and k == 0, stop=False,
                                         skip_group_check=True)
                    for k in range(KPS):
                        tile = KPS * js + k
                        nc.tensor.matmul(UB[DK * k:DK * (k + 1), :], TT[:, tile, 0, :],
                                         Pl[:, s % RING, QB * k:QB * (k + 1)], start=False, stop=js == SPB - 1,
                                         skip_group_check=True)
                    for i in range(4):
                        part = (Ph, Pl)[i // 2]
                        last = nc.tensor.matmul(SUMB[32 * i:32 * (i + 1), :], ones16[:, :],
                                                part[:, s % RING, QB * (i % 2):QB * (i % 2 + 1)],
                                                start=js == 0, stop=js == SPB - 1)
                    last.then_inc(product_done, 1)
                if has_maxima(t):
                    maxima(at, 1)
                for job, n, i in side_jobs(t):
                    if side.n:
                        pe.wait_ge(side_free, side.value(at))
                    side.add(at)
                    if job == "maxima":
                        pe.wait_ge(nm_ready, at.value(n_of(at, n) + 1, 2 * NQB))
                        last = transpose(SIDE[0:2 * TPB, 0:P], nm_parts[:, :, :].rearrange("p a t -> p (a t)"))
                    elif job in "kq":
                        if job == "k" and i == 0:
                            pe.wait_ge(weights_ready, at.value(n - (0 if at.turn is None else 2), 2))
                        last = project(SIDE, 2 if job == "k" else 0, TK if job == "k" else TQ, i)
                    elif job == "sums":
                        pe.wait_ge(u_free, at.value(n_of(at, n) + 1, 2 * NQB))
                        for q in range(TPB):
                            last = nc.tensor.matmul(SIDE[:, 2 * q:2 * q + 2], sums[:, P * q:P * (q + 1)],
                                                    quarter[:, :], start=True, stop=True)
                    else:
                        head = head_of(at, n // NQB)
                        for q in range(TPB):
                            last = nc.tensor.matmul(SIDE[:, P * q:P * (q + 1)], U[:, P * q:P * (q + 1)],
                                                    GG[:, bass.ds(head * EMBED, EMBED)], start=True, stop=True)
                    last.then_inc(side_full, 1)

            run_steps(nc.tensor, step)
            pe.wait_ge(side_free, side.n)
            ffn(1, gen[0])


_INPUTS = ("z", "wq", "wk", "wv", "fcq_w", "fcq_b", "fck_w", "fck_b", "fcv_w", "fcv_b", "fco_w", "fco_b")
_FFN = ("w_gate", "w_up", "w_down")


def kernel(**inputs):
    import numpy as np
    import concourse.bacc as bacc
    from concourse.bass_utils import run_bass_kernel_spmd

    nc = bacc.Bacc("TRN2", target_bir_lowering=False, num_devices=1)
    arrays, args = {}, {}
    for name in _INPUTS + _FFN:
        a = np.ascontiguousarray(inputs[("L0_attn_" if name in _INPUTS else "L0_ffn_") + name])
        arrays[f"in_{name}"] = a
        args[name] = nc.dram_tensor(f"in_{name}", a.shape, mybir.dt.from_np(a.dtype), kind="ExternalInput").ap()
    args["out"] = nc.dram_tensor("out", (1, SEQ, EMBED), F32, kind="ExternalOutput").ap()
    build(nc, **args)
    result = run_bass_kernel_spmd(nc, [arrays], core_ids=[0])
    return result.results[0]["out"]
```

```python
from contextlib import ExitStack

import concourse.bass as bass
from concourse import mybir

F32 = mybir.dt.float32
F32R = mybir.dt.float32r
F16 = mybir.dt.float16
I32 = mybir.dt.int32
ALU = mybir.AluOpType
ACT = mybir.ActivationFunctionType
AXX = mybir.AxisListType.X

P = 128
SEQ, EMBED, HIDDEN = 2048, 128, 384
HEADS, DK = 16, 64
EPS = 1e-5
SCALE = 1.0 / 127.0
T_RANGE = 4096.0

TILES = SEQ // P
QB = 512
NQB = SEQ // QB
TPB = QB // P
KPS = 2
SPB = TILES // KPS
HC = HIDDEN // P
G_ALL = HEADS * NQB
STEPS = G_ALL * SPB
AHEAD = 2
LAG = 3
PAIR = 2 * NQB * SPB
FIRST = 6
ROUNDS = HEADS // 2 - 1
RING = 4

FFN_ORDER = [("T", 0), ("T", 1), ("H", 0), ("T", 2), ("H", 1), ("D", 0), ("T", 3), ("H", 2), ("D", 1),
             ("H", 3), ("D", 2), ("D", 3)]


PROJECTIONS = {(0, 2): ("k", 0), (0, 7): ("k", 1), (1, 2): ("k", 2), (1, 4): ("k", 3), (1, 7): ("q", 0),
               (2, 2): ("q", 1), (2, 7): ("q", 2), (3, 2): ("q", 3)}


def side_jobs(t):
    g, j = divmod(t, SPB)
    h, b = divmod(g, NQB)
    jobs = []
    if j == 1 and g + 1 < G_ALL:
        jobs.append(("maxima", g + 1, 0))
    if (b, j) in PROJECTIONS and h + 1 < HEADS:
        what, i = PROJECTIONS[b, j]
        jobs.append((what, h + 1, i))
    if j == LAG and g >= 1:
        jobs.append(("sums", g - 1, 0))
    if j == LAG + 2 and g >= 1:
        jobs.append(("out", g - 1, 0))
    return jobs


def has_scores(t):
    return t < STEPS


def has_product(t):
    return LAG <= t < STEPS + LAG


def has_maxima(t):
    return t < STEPS - AHEAD * SPB


JOBS_PER_PAIR = sum(2 + len(side_jobs(PAIR + t)) for t in range(PAIR))


def jobs_through(t, job):
    before = sum(2 * has_maxima(u) + len(side_jobs(u)) for u in range(t))
    return before + has_maxima(t) + [what for what, _, _ in side_jobs(t)].index(job) + 1


assert JOBS_PER_PAIR % 2 == 0
CHAIN_PER_PAIR = 2 * (NQB + NQB) + 2 * (2 * NQB) + 2 * NQB


class Turn:

    def __init__(self, local, turn, absolute):
        self.local = local
        self.turn = turn
        self.absolute = absolute

    def value(self, n, per_pair):
        return n if self.turn is None else self.turn * per_pair + n

    def t(self, offset=0):
        return self.value(self.local + offset, PAIR)


def run_steps(engine, step):
    for n in range(FIRST):
        step(Turn(n, None, n))
    with engine.Fori(0, ROUNDS) as turn:
        for n in range(FIRST, FIRST + PAIR):
            step(Turn(n, turn, n + PAIR))
    for n in range(ROUNDS * PAIR + FIRST, STEPS + SPB):
        step(Turn(n, None, n))


class Count:

    def __init__(self, per_pair):
        self.n = 0
        self.per_pair = per_pair
        self.entered = None

    def add(self, at):
        if at.turn is not None and self.entered is None:
            self.entered = self.n
        if at.turn is None and self.entered is not None:
            assert self.n == self.entered + self.per_pair, (self.n, self.entered, self.per_pair)
            self.n = self.entered + ROUNDS * self.per_pair
            self.entered = None
        self.n += 1

    def count(self, at):
        if at.turn is None and self.entered is not None:
            return self.entered + ROUNDS * self.per_pair
        return self.n

    def value(self, at, n=None):
        return at.value(self.n if n is None else n, self.per_pair)


def build(nc, z, wq, wk, wv, fcq_w, fcq_b, fck_w, fck_b, fcv_w, fcv_b, fco_w, fco_b, w_gate, w_up, w_down,
          out):
    ctx = ExitStack()
    with ctx:
        def sb(name, shape, dt=F32):
            return ctx.enter_context(nc.sbuf_tensor(name, shape, dt))

        def sem(name):
            return ctx.enter_context(nc.semaphore(name))

        X = sb("X", [P, TILES, EMBED])
        XN = sb("XN", [P, TILES, EMBED])
        XT = sb("XT", [P, SEQ])
        OUT = XN
        stats = sb("stats", [P, TILES, 6])
        meanvar = sb("meanvar", [P, TILES, 2])
        std = sb("std", [P, TILES])
        rstd = sb("rstd", [P, TILES])
        ident = sb("ident", [P, P])
        ones = sb("ones", [P, P])
        ones16 = sb("ones16", [P, 32], F16)
        epsc = sb("epsc", [P, 1])
        w_int = sb("w_int", [P, 3, HIDDEN], I32)
        w_deq = sb("w_deq", [P, 3, HIDDEN])
        w_t = sb("w_t", [P, 3, HIDDEN])
        work = sb("work", [P, 2 * HC * QB])
        hT = work[:, :].rearrange("p (r c q) -> p r c q", r=2, c=HC)
        Pf = work[:, 0:2 * KPS * QB].rearrange("p (r n) -> p r n", r=2)
        sg = sb("sg", [P, 2, QB])
        w_in = sb("w_in", [P, 3, 2, DK])
        fqk = sb("fqk", [P, 2 * HEADS * DK])
        fq, fk = (fqk[:, i * HEADS * DK:(i + 1) * HEADS * DK].rearrange("p (h d) -> p h d", h=HEADS)
                  for i in range(2))
        Pl = fqk[:, :].bitcast(F16).rearrange("p (r n) -> p r n", r=RING)
        fv = sb("fv", [DK, HEADS * DK])
        fvT = sb("fvT", [P, HEADS // 2, 2, DK])
        fo_u = sb("fo_u", [P, HEADS // 2 * EMBED])
        fo = fo_u[:, :].rearrange("p (c e) -> p c e", e=EMBED)
        U, sums = fo_u[:, 0:QB], fo_u[:, QB:2 * QB]
        b_rows = sb("b_rows", [HEADS, 4, DK])
        bv_rows = sb("bv_rows", [HEADS // 2, P])
        bo_row = sb("bo_row", [1, EMBED])
        bqk = sb("bqk", [P, HEADS, 2])
        bh = sb("bh", [P, 2])
        bv = sb("bv", [P, HEADS // 2])
        W4 = sb("W4", [P, HEADS, 4, DK], F32R)
        Wh = sb("Wh", [P, 4, 2, DK], F32R)
        TQ = sb("TQ", [P, SEQ], F32R)
        TK = sb("TK", [P, SEQ], F32R)
        TV = sb("TV", [P, SEQ])
        TT = sb("TT", [P, TILES, 2, DK], F16)
        amax = sb("amax", [P, 1])
        asafe = sb("asafe", [P, 1])
        arec = sb("arec", [P, 1])
        ascale = sb("ascale", [P, 1])
        aback = sb("aback", [P, 1])
        GG = sb("GG", [P, HEADS * EMBED])
        bout = sb("bout", [P, EMBED])
        KK = [sb(f"KK{i}", [P, SEQ], F32R) for i in range(2)]
        K1 = [sb(f"K1{i}", [P, SEQ], F32R) for i in range(2)]
        QQ = [sb(f"QQ{i}", [P, SEQ], F32R) for i in range(2)]
        QL = [sb(f"QL{i}", [P, SEQ], F32R) for i in range(2)]
        pm = sb("pm", [P, 2, TPB, TILES // TPB])
        nmax = sb("nmax", [P, TPB])
        nm_parts = sb("nm_parts", [P, 2, TPB])
        nm_rows = sb("nm_rows", [2 * TPB, P])
        Ph = sb("Ph", [P, RING, KPS * QB], F16)
        qsum = sb("qsum", [P, TPB])
        rsum = sb("rsum", [P, TPB])

        banks = ctx.enter_context(nc.psum_tensor("banks", [P, 8, QB], F32))
        S = [banks[:, 0:2, :], banks[:, 2:4, :]]
        UB, SUMB = banks[:, 6, :], banks[:, 7, :]
        JOB_BANKS = [banks[:, 4, :], banks[:, 5, :]]
        gate_banks = [banks[:, 0, :], banks[:, 1, :]]
        up_banks = [banks[:, 2, :], banks[:, 3, :]]
        gen_banks = [banks[:, i, :] for i in range(4, 8)]

        x_in = [sem(f"x_in{i}") for i in range(NQB)]
        wffn_in, watt_in, wfc_in = sem("wffn_in"), sem("watt_in"), sem("wfc_in")
        const_ready = sem("const_ready")
        dve_chain = sem("dve_chain")
        deq_ready = sem("deq_ready")
        stats_ready, std_ready, xn_ready = sem("stats_ready"), sem("std_ready"), sem("xn_ready")
        gen_full, gen_free = sem("gen_full"), sem("gen_free")
        gate_full, silu_ready = sem("gate_full"), sem("silu_ready")
        up_full, h_ready = sem("up_full"), sem("h_ready")
        tv_ready, bout_ready, x_biased = sem("tv_ready"), sem("bout_ready"), sem("x_biased")
        first_max_full, first_max_free = sem("first_max_full"), sem("first_max_free")
        scores_ready, exp_done, lo_ready, product_done = (
            sem("scores_ready"), sem("exp_done"), sem("lo_ready"), sem("product_done"))
        job_full, job_free = sem("job_full"), sem("job_free")
        u_free = sem("u_free")
        nm_ready, nm_rows_ready, nm_written = sem("nm_ready"), sem("nm_rows_ready"), sem("nm_written")
        dve_loop = sem("dve_loop")
        k_hi_written = sem("k_hi_written")
        weights_ready = sem("weights_ready")
        out_ready, stored = sem("out_ready"), sem("stored")

        W_FILLS = 5
        FFN_FILLS = 2 * NQB
        K_EVACUATED = W_FILLS + FFN_FILLS + NQB + 2 * NQB + NQB
        block = ctx.enter_context(nc.Block())

        def write_k_hi(sp, h, emptied, count):
            sp.wait_ge(emptied, count)
            sp.dma_start(K1[h % 2][0:DK, :].bitcast(F32), KK[h % 2][0:DK, :].bitcast(F32)).then_inc(k_hi_written, 16)

        def write_maxima_rows(sp, g, count):
            sp.wait_ge(nm_rows_ready, count)
            ql = QL[g // NQB % 2]
            b = g % NQB
            sp.dma_start(ql[DK:DK + 2, QB * b:QB * (b + 1)].bitcast(F32), nm_rows[:, :]).then_inc(nm_written, 16)

        def n_of(at, g):
            return g if at.turn is None else g - 2 * NQB

        def head_of(at, h):
            return h if at.turn is None else at.turn * 2 + (h - 2)

        def stage_weights(head):
            own = bass.ds(head, 1)
            for twice in range(2):
                nc.vector.tensor_copy(Wh[:, :, twice, :],
                                      W4[:, own, :, :].bitcast(F32).rearrange("p o a d -> p (o a) d"))
            return nc.vector.tensor_copy(bh[:, :], bqk[:, own, :].rearrange("p o a -> p (o a)"))

        def evacuate_k(h, b, full, link_):
            own = slice(QB * b, QB * (b + 1))
            kk = KK[h % 2]
            link_(nc.vector.tensor_scalar(kk[:, own], full, bh[:, 1:2], None, ALU.add))
            return nc.vector.scalar_tensor_tensor(kk[DK:P, own], full[DK:P, :], bh[DK:P, 1:2],
                                                  kk[DK:P, own].bitcast(F32), ALU.add, ALU.subtract)

        def evacuate_q(h, b, full, link_):
            own = slice(QB * b, QB * (b + 1))
            qq, ql = QQ[h % 2], QL[h % 2]
            link_(nc.vector.tensor_scalar(qq[:, own], full, bh[:, 0:1], None, ALU.add))
            return nc.vector.scalar_tensor_tensor(ql[0:DK, own], full[0:DK, :], bh[0:DK, 0:1],
                                                  qq[0:DK, own].bitcast(F32), ALU.add, ALU.subtract)

        def negate_maxima(g, link_):
            link_(nc.vector.tensor_reduce(nmax[:, :], pm[:, g % 2, :, :], AXX, ALU.max, negate=True))
            link_(nc.vector.tensor_copy(nm_parts[:, 0, :].bitcast(F32R), nmax[:, :]))
            return nc.vector.tensor_tensor(nm_parts[:, 1, :].bitcast(F32R), nmax[:, :], nm_parts[:, 0, :],
                                           ALU.subtract)

        @block.sync
        def _(sp):
            z_view = z.rearrange("o (b t p) d -> b p (o t) d", p=P, t=TPB)
            for b in range(NQB):
                sp.dma_start(X[:, TPB * b:TPB * (b + 1), :], z_view[b]).then_inc(x_in[b], 16)
            for i, w in enumerate((wq, wk, wv)):
                for twice in range(2):
                    sp.dma_start(w_in[:, i, twice, :], w).then_inc(watt_in, 16)
            sp.wait_ge(const_ready, 10)
            write_k_hi(sp, 0, gen_free, K_EVACUATED)
            def rows_of_block(g, turn):
                write_maxima_rows(sp, g, g + 1 if turn is None else turn * (2 * NQB) + (g + 1))
                h, b = divmod(g, NQB)
                if b == 2 and h + 1 < HEADS:
                    kb, kj = next(at for at, (what, i) in PROJECTIONS.items() if (what, i) == ("k", NQB - 1))
                    n = jobs_through((h * NQB + kb) * SPB + kj, "k")
                    write_k_hi(sp, h + 1, job_free, n if turn is None else turn * JOBS_PER_PAIR + n)

            rows_of_block(0, None)
            with sp.Fori(0, ROUNDS) as turn:
                for g in range(1, 1 + 2 * NQB):
                    rows_of_block(g, turn)
            for g in range(1 + ROUNDS * 2 * NQB, G_ALL):
                rows_of_block(g, None)
            out_view = out.rearrange("o (b t p) d -> b p (o t) d", p=P, t=TPB)
            for b in range(NQB):
                sp.wait_ge(out_ready, b + 1)
                sp.dma_start(out_view[b], OUT[:, TPB * b:TPB * (b + 1), :]).then_inc(stored, 16)
            sp.wait_ge(stored, 16 * NQB)

        @block.gpsimd
        def _(pool):
            def fill(ins, n):
                ins.then_inc(const_ready, 1)
                pool.wait_ge(const_ready, n)

            fill(nc.gpsimd.memset(ident[:, :], 0.0), 1)
            fill(nc.gpsimd.affine_select(out=ident[:, :], in_=ident[:, :], compare_op=ALU.not_equal, fill=1.0,
                                         base=0, pattern=[[-1, P]], channel_multiplier=1), 2)
            fill(nc.gpsimd.memset(ones[:, :], 1.0), 3)
            fill(nc.gpsimd.memset(ones16[:, :], 1.0), 4)
            for i in range(2):
                fill(nc.gpsimd.memset(QL[i][DK:P, :].bitcast(F32), 0.0), 5 + 3 * i)
                fill(nc.gpsimd.memset(K1[i][DK:P, :].bitcast(F32), 0.0), 6 + 3 * i)
                fill(nc.gpsimd.memset(K1[i][DK:DK + 2, :].bitcast(F32), 1.0), 7 + 3 * i)
            pool.wait_ge(bout_ready, 1)
            pool.wait_ge(xn_ready, 2 * NQB)
            for t in range(TILES):
                nc.gpsimd.tensor_tensor(X[:, t, :], X[:, t, :], bout[:, :], ALU.add).then_inc(x_biased, 1)

            def step(at):
                t = at.absolute
                if not has_scores(t):
                    return
                pool.wait_ge(exp_done, at.t(1))
                if t >= RING:
                    pool.wait_ge(product_done, at.t(1 - RING))
                nc.gpsimd.tensor_tensor(Pl[:, t % RING, :], Pf[:, t % 2, :], Ph[:, t % RING, :],
                                        ALU.subtract).then_inc(lo_ready, 1)

            run_steps(nc.gpsimd, step)

        @block.scalar
        def _(act):
            for i, w in enumerate((w_gate, w_up)):
                act.dma_start(w_int[:, i, :].rearrange("p (c d) -> p c d", c=HC),
                              w.rearrange("(c p) d -> p c d", p=P)).then_inc(wffn_in, 16)
            act.dma_start(w_int[:, 2, :], w_down).then_inc(wffn_in, 16)
            for rows, w in ((b_rows[:, 0, :], fcq_b), (b_rows[:, 1, :], fcq_b),
                            (b_rows[:, 2, :], fck_b), (b_rows[:, 3, :], fck_b)):
                act.dma_start(rows, w.rearrange("(h d) -> h d", d=DK)).then_inc(wfc_in, 16)
            act.dma_start(bv_rows[:, :], fcv_b.rearrange("(h d) -> h d", d=P)).then_inc(wfc_in, 16)
            act.dma_start(bo_row[:, :], fco_b.rearrange("(o d) -> o d", o=1)).then_inc(wfc_in, 16)
            act.dma_start(fv[:, :], fcv_w).then_inc(wfc_in, 16)
            act.dma_start(fo[:, :, :], fco_w.rearrange("(c p) e -> p c e", p=P)).then_inc(wfc_in, 16)
            for f, w in ((fq, fcq_w), (fk, fck_w)):
                for half in range(2):
                    act.dma_start(f[DK * half:DK * (half + 1), :, :].rearrange("p h d -> p (h d)"),
                                  w).then_inc(wfc_in, 16)

            def layer_norm(n):
                act.wait_ge(stats_ready, n + 1)
                nc.scalar.activation(std[:, :], meanvar[:, :, 1], ACT.Sqrt, bias=epsc[:, :]).then_inc(std_ready, 1)

            def ffn(n):
                for b in range(NQB):
                    for c in range(HC):
                        k = (n * NQB + b) * HC + c
                        act.wait_ge(gate_full, k + 1)
                        if k >= 2:
                            act.wait_ge(h_ready, k - 1)
                        nc.scalar.activation(sg[:, k % 2, :], gate_banks[k % 2], ACT.Silu).then_inc(silu_ready, 1)

            layer_norm(0)
            ffn(0)
            layer_norm(1)

            def step(at):
                t = at.absolute
                if not has_scores(t):
                    return
                act.wait_ge(scores_ready, at.t(1))
                if t >= RING:
                    act.wait_ge(product_done, at.t(1 - RING))
                scores = S[t % 2]
                nc.scalar.activation(Ph[:, t % RING, :].rearrange("p (k q) -> p k q", k=KPS), scores, ACT.Exp)
                if t >= 2:
                    act.wait_ge(lo_ready, at.t(-1))
                nc.scalar.activation(Pf[:, t % 2, :].rearrange("p (k q) -> p k q", k=KPS), scores,
                                     ACT.Exp).then_inc(exp_done, 1)

            def step_and_products(at):
                step(at)
                t = at.absolute
                if t % SPB == LAG - 1 and SPB <= t < STEPS + SPB:
                    act.wait_ge(product_done, at.t(1 - LAG))
                    nc.scalar.copy(U, UB)
                    nc.scalar.copy(sums, SUMB).then_inc(u_free, 1)

            run_steps(nc.scalar, step_and_products)
            layer_norm(2)
            ffn(1)

        @block.vector
        def _(dve):
            chained = [0]
            gen = [0]

            def link(ins):
                chained[0] += 1
                ins.then_inc(dve_chain, 1)
                dve.wait_ge(dve_chain, chained[0])

            def take():
                gen[0] += 1
                dve.wait_ge(gen_full, gen[0])
                return gen_banks[(gen[0] - 1) % 4]

            def layer_norm(n):
                for t in range(TILES):
                    if n == 0 and t % TPB == 0:
                        dve.wait_ge(x_in[t // TPB], 16)
                    last = nc.vector.bn_stats(stats[:, t, :], X[:, t, :])
                link(last)
                for t in range(TILES):
                    last = nc.vector.bn_aggr(meanvar[:, t, :], stats[:, t, :])
                last.then_inc(stats_ready, 1)
                dve.wait_ge(stats_ready, n + 1)
                dve.wait_ge(std_ready, n + 1)
                link(nc.vector.reciprocal(rstd[:, :], std[:, :]))
                for t in range(TILES):
                    ins = nc.vector.tensor_scalar(XN[:, t, :], X[:, t, :], meanvar[:, t, 0:1], rstd[:, t:t + 1],
                                                  ALU.subtract, ALU.mult)
                    if t % TPB == TPB - 1:
                        ins.then_inc(xn_ready, 1)

            def ffn(n):
                for what, b in FFN_ORDER:
                    if what == "T":
                        nc.vector.tensor_copy(XT[:, QB * b:QB * (b + 1)], take()).then_inc(gen_free, 1)
                    elif what == "H":
                        for c in range(HC):
                            k = (n * NQB + b) * HC + c
                            dve.wait_ge(up_full, k + 1)
                            dve.wait_ge(silu_ready, k + 1)
                            nc.vector.tensor_tensor(hT[:, b % 2, c, :], up_banks[k % 2], sg[:, k % 2, :],
                                                    ALU.mult).then_inc(h_ready, 1)
                    else:
                        full = take().rearrange("p (t d) -> p t d", t=TPB)
                        own = slice(TPB * b, TPB * (b + 1))
                        ins = nc.vector.scalar_tensor_tensor((X if n == 0 else OUT)[:, own, :], full, 0.5,
                                                             X[:, own, :], ALU.mult, ALU.add)
                        ins.then_inc(gen_free, 1)
                        if n == 1:
                            dve.wait_ge(gen_free, gen[0])
                            nc.vector.tensor_copy(rsum[:, 0:1], epsc[:, :]).then_inc(out_ready, 1)

            nc.vector.memset(epsc[:, :], EPS).then_inc(dve_chain, 1)
            chained[0] += 1
            dve.wait_ge(wffn_in, 16 * 3)
            for i in range(3):
                nc.vector.tensor_scalar(w_deq[:, i, :], w_int[:, i, :], SCALE, None, ALU.mult).then_inc(deq_ready, 1)
            layer_norm(0)
            for i in range(3):
                nc.vector.tensor_copy(w_t[:, i, :], take()[:, 0:HIDDEN]).then_inc(gen_free, 1)
            full = take()
            nc.vector.tensor_scalar(bqk[:, :, 0], full[:, 0:HEADS], DK ** -0.5, None, ALU.mult)
            nc.vector.tensor_copy(bqk[:, :, 1], full[:, HEADS:2 * HEADS])
            nc.vector.tensor_copy(bv[:, :], full[:, 2 * HEADS:2 * HEADS + HEADS // 2]).then_inc(gen_free, 1)
            full = take().rearrange("p (c d) -> p c d", c=HEADS // 2)
            nc.vector.tensor_copy(fvT[:, :, 0, :], full)
            nc.vector.tensor_copy(fvT[:, :, 1, :], full).then_inc(gen_free, 1)
            ffn(0)
            dve.wait_ge(gen_free, gen[0])
            layer_norm(1)
            for i, (f, scale) in enumerate(((fq, DK ** -0.5), (fk, 1.0))):
                link(nc.vector.tensor_scalar(W4[:, :, 2 * i, :], f[:, :, :], scale, None, ALU.mult))
                link(nc.vector.scalar_tensor_tensor(W4[:, :, 2 * i + 1, :], f[:, :, :], scale,
                                                    W4[:, :, 2 * i, :].bitcast(F32), ALU.mult, ALU.subtract))
            for b in range(NQB):
                nc.vector.tensor_copy(XT[:, QB * b:QB * (b + 1)], take()).then_inc(gen_free, 1)
            link(stage_weights(0))
            for T in (TK, TQ):
                for b in range(NQB):
                    full, own = take(), slice(QB * b, QB * (b + 1))
                    link(nc.vector.tensor_copy(T[:, own], full))
                    nc.vector.tensor_tensor(T[DK:P, own], full[DK:P, :], T[DK:P, own].bitcast(F32),
                                            ALU.subtract).then_inc(gen_free, 1)
            for b in range(NQB):
                evacuate_k(0, b, take(), link).then_inc(gen_free, 1)
            for b in range(NQB):
                evacuate_q(0, b, take(), link).then_inc(gen_free, 1)
            for i in range(AHEAD * TPB * 2):
                tile, half = divmod(i, 2)
                g, tile = divmod(tile, TPB)
                dve.wait_ge(first_max_full, i + 1)
                nc.vector.reduce_max(pm[:, g, tile, 2 * half:2 * half + 2], S[i % 2], AXX).then_inc(first_max_free, 1)
            dve.wait_ge(first_max_free, AHEAD * TPB * 2)
            negate_maxima(0, link).then_inc(nm_ready, 1)
            nc.vector.tensor_copy(nm_rows[:, :], take()[0:2 * TPB, 0:P]).then_inc(nm_rows_ready, 1)
            dve.wait_ge(nm_rows_ready, 1)
            nc.vector.tensor_copy(rsum[:, 0:1], epsc[:, :]).then_inc(gen_free, 1)
            for b in range(NQB):
                ins = nc.vector.tensor_copy(TV[:, QB * b:QB * (b + 1)], take())
                ins.then_inc(gen_free, 1)
            dve.wait_ge(gen_free, gen[0])
            link(nc.vector.tensor_reduce(amax[:, :], TV[:, :], AXX, ALU.max, apply_absolute_value=True))
            link(nc.vector.tensor_scalar(asafe[:, :], amax[:, :], 1e-30, None, ALU.max))
            link(nc.vector.reciprocal(arec[:, :], asafe[:, :]))
            link(nc.vector.tensor_scalar(ascale[:, :], arec[:, :], T_RANGE, None, ALU.mult))
            link(nc.vector.tensor_scalar(aback[:, :], asafe[:, :], 1.0 / T_RANGE, None, ALU.mult))
            nc.vector.tensor_scalar(TV[:, :], TV[:, :], ascale[:, :], None, ALU.mult).then_inc(tv_ready, 1)
            half_tiles = TILES // 2
            for i in range(2):
                full = take().rearrange("p (t d) -> p t d", t=half_tiles)
                own = slice(half_tiles * i, half_tiles * (i + 1))
                link(nc.vector.tensor_copy(TT[:, own, 0, :], full))
                nc.vector.tensor_tensor(TT[:, own, 1, :], full, TT[:, own, 0, :], ALU.subtract).then_inc(gen_free, 1)
            for i in range(4):
                own = GG[:, :].rearrange("p (a k r e) -> p a k r e", a=2, k=4, r=2)[:, i // 2, :, i % 2, :]
                nc.vector.tensor_scalar(own, take().rearrange("p (k e) -> p k e", k=4), aback[:, :], None,
                                        ALU.mult).then_inc(gen_free, 1)
            nc.vector.tensor_copy(bout[:, :], take()[:, 0:EMBED]).then_inc(gen_free, 1)
            dve.wait_ge(gen_free, gen[0])
            nc.vector.tensor_copy(rsum[:, 0:1], epsc[:, :]).then_inc(bout_ready, 1)

            jobs = Count(JOBS_PER_PAIR)
            chain = Count(CHAIN_PER_PAIR)
            sums_job = [0]

            def step(at):
                t = at.absolute
                g, j = divmod(t, SPB)
                b = g % NQB

                def loop_link(ins):
                    chain.add(at)
                    ins.then_inc(dve_loop, 1)
                    dve.wait_ge(dve_loop, chain.value(at))

                def take_job():
                    jobs.add(at)
                    dve.wait_ge(job_full, jobs.value(at))
                    return JOB_BANKS[(jobs.n - 1) % 2]

                def reduce_maxima(i):
                    chunk = 2 * (j % 2) + i
                    nc.vector.reduce_max(pm[:, g % 2, j // 2, chunk:chunk + 1], take_job(), AXX
                                         ).then_inc(job_free, 1)

                if j == 0 and g + 1 < G_ALL:
                    if g >= 1:
                        dve.wait_ge(job_free, jobs.value(at))
                    negate_maxima(g + 1, loop_link).then_inc(nm_ready, 1)
                if has_maxima(t):
                    reduce_maxima(0)
                for job, n, i in side_jobs(t):
                    SIDE = take_job()
                    if job == "maxima":
                        dve.wait_ge(nm_written, at.value(16 * n_of(at, n), 16 * 2 * NQB))
                        nc.vector.tensor_copy(nm_rows[:, :], SIDE[0:2 * TPB, 0:P]).then_inc(nm_rows_ready, 1)
                        dve.wait_ge(nm_rows_ready, at.value(n_of(at, n) + 1, 2 * NQB))
                        nc.vector.tensor_copy(amax[:, :], epsc[:, :]).then_inc(job_free, 1)
                    elif job == "k":
                        evacuate_k(n, i, SIDE, loop_link).then_inc(job_free, 1)
                    elif job == "q":
                        evacuate_q(n, i, SIDE, loop_link).then_inc(job_free, 1)
                    elif job == "sums":
                        loop_link(nc.vector.reduce_sum(qsum[:, :], SIDE.rearrange(
                            "p (t i o) -> p t i o", t=TPB, o=32)[:, :, :, 0], AXX))
                        nc.vector.reciprocal(rsum[:, :], qsum[:, :]).then_inc(job_free, 1)
                        sums_job[0] = jobs.n
                    else:
                        dve.wait_ge(job_free, jobs.value(at, sums_job[0]))
                        if g == 1:
                            dve.wait_ge(x_biased, TILES)
                        for q in range(TPB):
                            tile = TPB * (n % NQB) + q
                            ins = nc.vector.scalar_tensor_tensor(X[:, tile, :], SIDE[:, P * q:P * (q + 1)],
                                                                 rsum[:, q:q + 1], X[:, tile, :], ALU.mult, ALU.add)
                        ins.then_inc(job_free, 1)
                if has_maxima(t):
                    reduce_maxima(1)
                if b == 3 and j == SPB - 1 and g // NQB + 2 < HEADS:
                    stage_weights(head_of(at, g // NQB + 2)).then_inc(weights_ready, 1)

            stage_weights(1).then_inc(weights_ready, 1)
            run_steps(nc.vector, step)
            dve.wait_ge(job_free, jobs.n)
            layer_norm(2)
            ffn(1)

        @block.tensor
        def _(pe):
            gen = [0]

            def give():
                gen[0] += 1
                if gen[0] > 4:
                    pe.wait_ge(gen_free, gen[0] - 4)
                return gen_banks[(gen[0] - 1) % 4]

            def transpose(to, of):
                k, m = of.shape
                return nc.tensor.transpose(to, of, ident[0:k, 0:k])

            def block_transposes(n, b):
                full = give()
                pe.wait_ge(xn_ready, n * NQB + b + 1)
                for i in range(TPB):
                    last = transpose(full[:, P * i:P * (i + 1)], XN[:, TPB * b + i, :])
                last.then_inc(gen_full, 1)

            def ffn(n, emptied):
                blocks_emptied = {}
                done = emptied
                for what, b in FFN_ORDER:
                    if what == "T":
                        block_transposes(2 * n if n else 0, b)
                        done += 1
                        blocks_emptied[b] = done
                    elif what == "H":
                        pe.wait_ge(gen_free, blocks_emptied[b])
                        for c in range(HC):
                            k = (n * NQB + b) * HC + c
                            if k >= 2:
                                pe.wait_ge(h_ready, k - 1)
                            for full, w, done_sem in ((gate_banks, 0, gate_full), (up_banks, 1, up_full)):
                                nc.tensor.matmul(full[k % 2], w_t[:, w, P * c:P * (c + 1)],
                                                 XT[:, QB * b:QB * (b + 1)], start=True, stop=True
                                                 ).then_inc(done_sem, 1)
                    else:
                        full = give()
                        done += 1
                        pe.wait_ge(h_ready, (n * NQB + b + 1) * HC)
                        for i in range(TPB):
                            for c in range(HC):
                                last = nc.tensor.matmul(full[:, P * i:P * (i + 1)],
                                                        hT[:, b % 2, c, P * i:P * (i + 1)],
                                                        w_t[:, 2, P * c:P * (c + 1)], start=c == 0, stop=c == HC - 1)
                        last.then_inc(gen_full, 1)

            def project(full, parts, T, b):
                for i in range(2):
                    last = nc.tensor.matmul(full, Wh[:, parts + i, :, :].rearrange("p a d -> p (a d)"),
                                            T[:, QB * b:QB * (b + 1)], start=i == 0, stop=i == 1)
                return last

            pe.wait_ge(const_ready, 2)
            for i in range(3):
                full = give()
                pe.wait_ge(deq_ready, i + 1)
                for c in range(HC):
                    last = transpose(full[:, P * c:P * (c + 1)], w_deq[:, i, P * c:P * (c + 1)])
                last.then_inc(gen_full, 1)
            full = give()
            pe.wait_ge(wfc_in, 16 * 12)
            transpose(full[:, 0:HEADS], b_rows[:, 0:2, :].rearrange("p a d -> p (a d)"))
            transpose(full[:, HEADS:2 * HEADS], b_rows[:, 2:4, :].rearrange("p a d -> p (a d)"))
            transpose(full[:, 2 * HEADS:2 * HEADS + HEADS // 2], bv_rows[:, :]).then_inc(gen_full, 1)
            full = give()
            for c in range(HEADS // 2):
                last = transpose(full[:, DK * c:DK * (c + 1)], fv[:, P * c:P * (c + 1)])
            last.then_inc(gen_full, 1)
            pe.wait_ge(gen_free, 3)
            ffn(0, W_FILLS)
            for b in range(NQB):
                block_transposes(1, b)
            base = gen[0]
            pe.wait_ge(watt_in, 16 * 6)

            def input_projection(i):
                for b in range(NQB):
                    full = give()
                    pe.wait_ge(gen_free, base - NQB + b + 1)
                    nc.tensor.matmul(full, w_in[:, i, :, :].rearrange("p a d -> p (a d)"),
                                     XT[:, QB * b:QB * (b + 1)], start=True, stop=True).then_inc(gen_full, 1)

            input_projection(1)
            input_projection(0)
            for parts, T, before in ((2, TK, base + NQB), (0, TQ, base + 2 * NQB)):
                for b in range(NQB):
                    full = give()
                    pe.wait_ge(gen_free, before - NQB + NQB - (NQB - 1 - b))
                    project(full, parts, T, b).then_inc(gen_full, 1)
            pe.wait_ge(gen_free, gen[0])
            for i in range(AHEAD * TPB * 2):
                tile, half = divmod(i, 2)
                if i >= 2:
                    pe.wait_ge(first_max_free, i - 1)
                for c in range(2):
                    keys = QB * (2 * half + c)
                    last = nc.tensor.matmul(S[i % 2][:, c, :], QQ[0][:, P * tile:P * (tile + 1)],
                                            KK[0][:, keys:keys + QB], start=True, stop=True)
                last.then_inc(first_max_full, 1)
            full = give()
            pe.wait_ge(nm_ready, 1)
            transpose(full[0:2 * TPB, 0:P], nm_parts[:, :, :].rearrange("p a t -> p (a t)")).then_inc(gen_full, 1)
            input_projection(2)
            pe.wait_ge(tv_ready, 1)
            for i in range(2):
                full = give()
                for t in range(TILES // 2):
                    tile = TILES // 2 * i + t
                    last = transpose(full[:, DK * t:DK * (t + 1)], TV[0:DK, P * tile:P * (tile + 1)])
                last.then_inc(gen_full, 1)
            for i in range(4):
                full = give()
                for k in range(4):
                    h = 8 * (i // 2) + 2 * k + i % 2
                    rows = slice(DK * (h % 2), DK * (h % 2 + 1))
                    last = nc.tensor.matmul(full[:, P * k:P * (k + 1)],
                                            fvT[rows, h // 2, :, :].rearrange("p a d -> p (a d)"),
                                            fo[rows, h // 2, :], start=True, stop=True)
                last.then_inc(gen_full, 1)
            full = give()
            pe.wait_ge(const_ready, 10)
            for c in range(HEADS // 2):
                nc.tensor.matmul(full[:, 0:EMBED], bv[:, c:c + 1].to_broadcast([P, P]), fo[:, c, :],
                                 start=c == 0, stop=False)
            nc.tensor.matmul(full[:, 0:EMBED], ones[0:1, :], bo_row[:, :], start=False, stop=True
                             ).then_inc(gen_full, 1)
            pe.wait_ge(gen_free, gen[0])
            pe.wait_ge(first_max_free, AHEAD * TPB * 2)

            jobs = Count(JOBS_PER_PAIR)

            def give_job(at):
                if jobs.n >= 2:
                    pe.wait_ge(job_free, at.value(jobs.count(at) - 1, JOBS_PER_PAIR))
                jobs.add(at)
                return JOB_BANKS[(jobs.n - 1) % 2]

            def maxima(at, i):
                t = at.absolute
                g, j = divmod(t, SPB)
                gm = g + AHEAD
                hm, bm = divmod(gm, NQB)
                tile = TPB * bm + j // 2
                keys = QB * (2 * (j % 2) + i)
                nc.tensor.matmul(give_job(at), QQ[hm % 2][:, P * tile:P * (tile + 1)], KK[hm % 2][:, keys:keys + QB],
                                 start=True, stop=True).then_inc(job_full, 1)

            def products_hi(at):
                s = at.absolute - LAG
                js = s % SPB
                pe.wait_ge(lo_ready, at.t(1 - LAG))
                if js == 0 and s >= SPB:
                    pe.wait_ge(u_free, at.value(n_of(at, s // SPB), 2 * NQB))
                for k in range(KPS):
                    tile = KPS * js + k
                    nc.tensor.matmul(UB, TT[:, tile, :, :].rearrange("p a d -> p (a d)"),
                                     Ph[:, s % RING, QB * k:QB * (k + 1)], start=js == 0 and k == 0, stop=False,
                                     skip_group_check=True)

            def products_lo(at):
                s = at.absolute - LAG
                js = s % SPB
                for k in range(KPS):
                    tile = KPS * js + k
                    nc.tensor.matmul(UB[DK * k:DK * (k + 1), :], TT[:, tile, 0, :],
                                     Pl[:, s % RING, QB * k:QB * (k + 1)], start=False, stop=js == SPB - 1,
                                     skip_group_check=True)
                for i in range(4):
                    part = (Ph, Pl)[i // 2]
                    last = nc.tensor.matmul(SUMB[32 * i:32 * (i + 1), :], ones16[:, :],
                                            part[:, s % RING, QB * (i % 2):QB * (i % 2 + 1)],
                                            start=js == 0, stop=js == SPB - 1)
                last.then_inc(product_done, 1)

            def step(at):
                t = at.absolute
                g, j = divmod(t, SPB)
                b, h = g % NQB, g // NQB
                if has_scores(t):
                    if j == 0 and b == 0:
                        pe.wait_ge(k_hi_written, at.value(16 * (h + 1 - (0 if at.turn is None else 2)), 16 * 2))
                    if j == 0:
                        pe.wait_ge(nm_written, at.value(16 * (n_of(at, g) + 1), 16 * 2 * NQB))
                    if t >= 2:
                        pe.wait_ge(exp_done, at.t(-1))
                    cols = slice(QB * b, QB * (b + 1))
                    for k in range(KPS):
                        tile = KPS * j + k
                        keys = slice(P * tile, P * (tile + 1))
                        nc.tensor.matmul(S[t % 2][:, k, :], KK[h % 2][:, keys], QQ[h % 2][:, cols],
                                         start=True, stop=False)
                        last = nc.tensor.matmul(S[t % 2][:, k, :], K1[h % 2][:, keys], QL[h % 2][:, cols],
                                                start=False, stop=True)
                    last.then_inc(scores_ready, 1)
                if has_maxima(t):
                    maxima(at, 0)
                if has_product(t):
                    products_hi(at)
                for job, n, i in side_jobs(t):
                    SIDE = give_job(at)
                    if job == "maxima":
                        pe.wait_ge(nm_ready, at.value(n_of(at, n) + 1, 2 * NQB))
                        last = transpose(SIDE[0:2 * TPB, 0:P], nm_parts[:, :, :].rearrange("p a t -> p (a t)"))
                    elif job in "kq":
                        if job == "k" and i == 0:
                            pe.wait_ge(weights_ready, at.value(n - (0 if at.turn is None else 2), 2))
                        last = project(SIDE, 2 if job == "k" else 0, TK if job == "k" else TQ, i)
                    elif job == "sums":
                        pe.wait_ge(u_free, at.value(n_of(at, n) + 1, 2 * NQB))
                        for q in range(TPB):
                            last = transpose(SIDE[:, P * q:P * (q + 1)], sums[:, P * q:P * (q + 1)])
                    else:
                        head = head_of(at, n // NQB)
                        for q in range(TPB):
                            last = nc.tensor.matmul(SIDE[:, P * q:P * (q + 1)], U[:, P * q:P * (q + 1)],
                                                    GG[:, bass.ds(head * EMBED, EMBED)], start=True, stop=True)
                    last.then_inc(job_full, 1)
                if has_product(t):
                    products_lo(at)
                if has_maxima(t):
                    maxima(at, 1)

            run_steps(nc.tensor, step)
            pe.wait_ge(job_free, jobs.n)
            ffn(1, gen[0])


_INPUTS = ("z", "wq", "wk", "wv", "fcq_w", "fcq_b", "fck_w", "fck_b", "fcv_w", "fcv_b", "fco_w", "fco_b")
_FFN = ("w_gate", "w_up", "w_down")


def kernel(**inputs):
    import numpy as np
    import concourse.bacc as bacc
    from concourse.bass_utils import run_bass_kernel_spmd

    nc = bacc.Bacc("TRN2", target_bir_lowering=False, num_devices=1)
    arrays, args = {}, {}
    for name in _INPUTS + _FFN:
        a = np.ascontiguousarray(inputs[("L0_attn_" if name in _INPUTS else "L0_ffn_") + name])
        arrays[f"in_{name}"] = a
        args[name] = nc.dram_tensor(f"in_{name}", a.shape, mybir.dt.from_np(a.dtype), kind="ExternalInput").ap()
    args["out"] = nc.dram_tensor("out", (1, SEQ, EMBED), F32, kind="ExternalOutput").ap()
    build(nc, **args)
    result = run_bass_kernel_spmd(nc, [arrays], core_ids=[0])
    return result.results[0]["out"]
```

```python
from contextlib import ExitStack

import concourse.bass as bass
from concourse import mybir

F32 = mybir.dt.float32
F32R = mybir.dt.float32r
F16 = mybir.dt.float16
I32 = mybir.dt.int32
ALU = mybir.AluOpType
ACT = mybir.ActivationFunctionType
AXX = mybir.AxisListType.X

P = 128
SEQ, EMBED, HIDDEN = 2048, 128, 384
HEADS, DK = 16, 64
EPS = 1e-5
SCALE = 1.0 / 127.0
T_RANGE = 4096.0

TILES = SEQ // P
QB = 512
NQB = SEQ // QB
TPB = QB // P
KPS = 2
SPB = TILES // KPS
HC = HIDDEN // P
G_ALL = HEADS * NQB
STEPS = G_ALL * SPB
AHEAD = 2
LAG = 3
PAIR = 2 * NQB * SPB
FIRST = 6
ROUNDS = HEADS // 2 - 1
WARMING = 18
SUM_ROWS = 3 * 32 + 1
RING = 4

GEN_BANKS = 4
EARLY = LAG


def each(*steps):
    return [(text.split()[0], int(text.split()[1])) for text in steps]


BEFORE = each(
    "stats0 0", "weights 0", "weights 1", "norm0 0", "weights 2", "stats0 1", "stats0 2", "T0 0", "norm0 1",
    "H0 0", "norm0 2", "T0 1", "H0 1", "H0 2", "T0 2", "stats0 3", "H0 3", "norm0 3", "H0 4", "D0 0", "T0 3",
    "H0 5", "stats1 0", "in_parts 0", "fc_parts 0",
    "H0 6", "norm1 0", "H0 7", "D0 1", "T1 0", "H0 8", "stats1 1", "fc_parts 1", "biases 0",
    "H0 9", "H0 10", "norm1 1", "D0 2", "H0 11", "stats1 2", "T1 1", "K 0",
    "D0 3", "norm1 2", "stage 0", "stats1 3", "K 1", "T1 2", "k 0", "Q 0", "norm1 3", "k 1", "V 0", "K 2", "q 0",
    "T1 3", "k 2", "V 1", "K 3", "Q 1", "V 2", "k 3", "Q 2", "V 3", "fcvT 0",
    *(f"M0 {i}" for i in range(5)), "Q 3", "bout 0", *(f"M0 {i}" for i in range(5, 2 * TPB)),
    "q 1", "nm 0", "scale 0",
    "M1 0", "M1 1", "M1 2", "M1 3", "q 2", "M1 4", "M1 5", "M1 6", "TT 0", "TT 1", "q 3", "M1 7", "M1 8", "G 0",
    "scores 0", "M1 9", "M1 10", "G 1", "M1 11", "scores 1", "M1 12", "G 2", "M1 13", "M1 14", "G 3", "M1 15",
    "scores 2")
AFTER_STEP = {STEPS: each("T2 0", "T2 1"), STEPS + 1: each("H2 0", "H2 1"),
              STEPS + LAG - 1: each("H2 2"), STEPS + LAG: each("T2 2", "H2 3"),
              STEPS + LAG + 2: each("H2 4", "D2 0", "stats2 3")}
AFTER_ALL = each("H2 5", "H2 6", "norm2 3", "H2 7", "T2 3", "D2 1", "H2 8", "H2 9", "H2 10",
                 "H2 11", "D2 2", "D2 3")
AFTER = [step for steps in AFTER_STEP.values() for step in steps] + AFTER_ALL
NO_BANK = ("stats0", "norm0", "stats1", "norm1", "stats2", "norm2", "H0", "H2", "in_parts", "fc_parts", "stage",
           "M0", "scale", "scores")
FILLS = [step for step in BEFORE if step[0] not in NO_BANK]
FILLS += [None] * (-len(FILLS) % GEN_BANKS)
FILLS += [step for step in AFTER if step[0] not in NO_BANK]


def bank_and_use(what, i):
    n = FILLS.index((what, i))
    bank = n % GEN_BANKS
    return bank, sum(step is not None for step in FILLS[bank:n + 1:GEN_BANKS])


def last_uses(steps):
    fills = sum(what not in NO_BANK for what, _ in steps)
    return [(fills - bank + GEN_BANKS - 1) // GEN_BANKS for bank in range(GEN_BANKS)]


NORMS = [step for step in BEFORE if step[0] in ("norm0", "norm1")] + each(*(f"norm2 {b}" for b in range(NQB)))
HIDDEN_STEPS = [step for step in BEFORE + AFTER if step[0] in ("H0", "H2")]
HI_STEPS = [step for step in BEFORE + AFTER if step[0] in ("T0", "T1", "T2", "in_parts", "fc_parts", "K", "Q",
                                                           "k", "q", "TT")]
LAST_STATS = {STEPS - (NQB - 1 - b) * SPB + LAG + 3: b for b in range(NQB - 1)}
LAST_RSTD = {t + 1: b for t, b in LAST_STATS.items()}
LAST_NORM = {t + 3: b for t, b in LAST_STATS.items()}


def lo_halves(t):
    return t - (STEPS - AHEAD * SPB) + 1


def lo_shared(t):
    return STEPS - AHEAD * SPB <= t < STEPS


PROJECTIONS = {(0, 2): ("k", 0), (0, 7): ("k", 1), (1, 2): ("k", 2), (1, 4): ("k", 3), (1, 6): ("q", 0),
               (2, 2): ("q", 1), (2, 7): ("q", 2), (3, 2): ("q", 3)}


def side_jobs(t):
    g, j = divmod(t, SPB)
    h, b = divmod(g, NQB)
    jobs = []
    if j == 1 and g + 1 < G_ALL:
        jobs.append(("maxima", g + 1, 0))
    if (b, j) in PROJECTIONS and h + 1 < HEADS:
        what, i = PROJECTIONS[b, j]
        jobs.append((what, h + 1, i))
    if j == LAG and g >= 1:
        jobs.append(("sums", g - 1, 0))
    if j == LAG + 2 and g >= 1:
        jobs.append(("out", g - 1, 0))
    return jobs


def has_scores(t):
    return t < STEPS


def has_product(t):
    return LAG <= t < STEPS + LAG


def has_maxima(t):
    return t < STEPS - AHEAD * SPB


JOBS_PER_PAIR = sum(2 + len(side_jobs(PAIR + t)) for t in range(PAIR))
assert JOBS_PER_PAIR % 2 == 0
CHAIN_PER_PAIR = 2 * (NQB + NQB) + 2 * (2 * NQB) + 2 * NQB


class Turn:

    def __init__(self, local, turn, absolute):
        self.local = local
        self.turn = turn
        self.absolute = absolute

    def value(self, n, per_pair):
        return n if self.turn is None else self.turn * per_pair + n

    def t(self, offset=0):
        return self.value(self.local + offset, PAIR)


def run_steps(engine, step):
    for n in range(FIRST):
        step(Turn(n, None, n))
    with engine.Fori(0, ROUNDS) as turn:
        for n in range(FIRST, FIRST + PAIR):
            step(Turn(n, turn, n + PAIR))
    for n in range(ROUNDS * PAIR + FIRST, STEPS + SPB):
        step(Turn(n, None, n))


class Count:

    def __init__(self, per_pair):
        self.n = 0
        self.per_pair = per_pair
        self.entered = None

    def add(self, at):
        if at.turn is not None and self.entered is None:
            self.entered = self.n
        if at.turn is None and self.entered is not None:
            assert self.n == self.entered + self.per_pair, (self.n, self.entered, self.per_pair)
            self.n = self.entered + ROUNDS * self.per_pair
            self.entered = None
        self.n += 1

    def count(self, at):
        if at.turn is None and self.entered is not None:
            return self.entered + ROUNDS * self.per_pair
        return self.n

    def value(self, at, n=None):
        return at.value(self.n if n is None else n, self.per_pair)


def build(nc, z, wq, wk, wv, fcq_w, fcq_b, fck_w, fck_b, fcv_w, fcv_b, fco_w, fco_b, w_gate, w_up, w_down,
          out):
    ctx = ExitStack()
    with ctx:
        def sb(name, shape, dt=F32):
            return ctx.enter_context(nc.sbuf_tensor(name, shape, dt))

        def sem(name):
            return ctx.enter_context(nc.semaphore(name))

        X = sb("X", [P, TILES, EMBED])
        XN = sb("XN", [P, TILES, EMBED])
        XT = sb("XT", [P, SEQ], F32R)
        OUT = XN
        stats = sb("stats", [P, TILES, 6])
        meanvar = sb("meanvar", [P, TILES, 2])
        var_eps = sb("var_eps", [P, TILES])
        signal = sb("signal", [P, 1])
        rstd = sb("rstd", [P, TILES])
        ident = sb("ident", [P, P])
        ones = sb("ones", [P, P])
        ones16 = sb("ones16", [P, 32], F16)
        warm = sb("warm", [P, 1])
        epsc = sb("epsc", [P, TPB])
        minus_half = sb("minus_half", [P, TPB])
        w_t = sb("w_t", [P, 2, HIDDEN], F32R)
        w_down_t = sb("w_down_t", [P, HIDDEN])
        work = sb("work", [P, 2 * HC * QB])
        w_int, w_f = (work[:, i * 3 * HIDDEN:(i + 1) * 3 * HIDDEN].rearrange("p (w n) -> p w n", w=3)
                      for i in range(2))
        w_int = w_int.bitcast(I32)
        hT = work[:, :].rearrange("p (r c q) -> p r c q", r=2, c=HC)
        Pf = work[:, 0:2 * KPS * QB].rearrange("p (r n) -> p r n", r=2)
        sg = sb("sg", [P, 2, QB])
        w_in = sb("w_in", [P, 3, 2, DK])
        w_parts = sb("w_parts", [P, 2, 3, 2 * DK], F32R)
        fqk = sb("fqk", [P, 2 * HEADS * DK])
        fq, fk = (fqk[:, i * HEADS * DK:(i + 1) * HEADS * DK].rearrange("p (h d) -> p h d", h=HEADS)
                  for i in range(2))
        Pl = fqk[:, :].bitcast(F16).rearrange("p (r n) -> p r n", r=RING)
        fv = sb("fv", [DK, HEADS * DK])
        fvT = sb("fvT", [P, HEADS // 2, 2, DK])
        fo_u = sb("fo_u", [P, HEADS // 2 * EMBED])
        fo = fo_u[:, :].rearrange("p (c e) -> p c e", e=EMBED)
        U, sums = fo_u[:, 0:QB], fo_u[:, QB:2 * QB]
        b_rows = sb("b_rows", [HEADS, 4, DK])
        bv_rows = sb("bv_rows", [HEADS // 2, P])
        bo_row = sb("bo_row", [1, EMBED])
        bqk = sb("bqk", [P, HEADS, 2])
        bh = sb("bh", [P, 2])
        bv = sb("bv", [P, HEADS // 2])
        W4 = sb("W4", [P, HEADS, 4, DK], F32R)
        Wh = sb("Wh", [P, 4, 2, DK], F32R)
        TQ = sb("TQ", [P, SEQ], F32R)
        TK = sb("TK", [P, SEQ], F32R)
        TV = sb("TV", [P, SEQ])
        TT = sb("TT", [P, TILES, 2, DK], F16)
        amax = sb("amax", [P, 1])
        amax_by = sb("amax_by", [P, NQB])
        asafe = sb("asafe", [P, 1])
        arec = sb("arec", [P, 1])
        ascale = sb("ascale", [P, 1])
        aback = sb("aback", [P, 1])
        GG = sb("GG", [P, HEADS * EMBED])
        bout = sb("bout", [P, EMBED])
        KK = [sb(f"KK{i}", [P, SEQ], F32R) for i in range(2)]
        K1 = [sb(f"K1{i}", [P, SEQ], F32R) for i in range(2)]
        QQ = [sb(f"QQ{i}", [P, SEQ], F32R) for i in range(2)]
        XTL = QQ[1]
        QL = [sb(f"QL{i}", [P, SEQ], F32R) for i in range(2)]
        pm = sb("pm", [P, 2, TPB, TILES // TPB])
        nmax = sb("nmax", [P, TPB])
        nm_parts = sb("nm_parts", [P, 2, TPB])
        nm_rows = sb("nm_rows", [2 * TPB, P])
        Ph = sb("Ph", [P, RING, KPS * QB], F16)
        qsum = sb("qsum", [P, TPB])
        rsum = sb("rsum", [P, TPB])

        banks = ctx.enter_context(nc.psum_tensor("banks", [P, 8, QB], F32))
        S = [banks[:, 0:2, :], banks[:, 2:4, :]]
        UB, SUMB = banks[:, 6, :], banks[:, 7, :]
        JOB_BANKS = [banks[:, 4, :], banks[:, 5, :]]
        gate_banks = [banks[:, 0, :], banks[:, 1, :]]
        up_banks = [banks[:, 2, :], banks[:, 3, :]]
        gen_banks = [banks[:, i, :] for i in range(4, 8)]

        x_in = [sem(f"x_in{i}") for i in range(NQB)]
        wffn_in = [sem(f"wffn_in{i}") for i in range(3)]
        watt_in, wfc_in = sem("watt_in"), sem("wfc_in")
        const_ready = sem("const_ready")
        dve_chain = sem("dve_chain")
        deq_ready = sem("deq_ready")
        stats_ready, rstd_ready, xn_ready = sem("stats_ready"), sem("rstd_ready"), sem("xn_ready")
        pool_chain = sem("pool_chain")
        gen_full = [sem(f"gen_full{i}") for i in range(GEN_BANKS)]
        gen_free = [sem(f"gen_free{i}") for i in range(GEN_BANKS)]
        hi_ready = sem("hi_ready")
        parts_ready = sem("parts_ready")
        fc_ready = sem("fc_ready")
        fq_split = sem("fq_split")
        scale_ready = sem("scale_ready")
        gate_full, silu_ready = sem("gate_full"), sem("silu_ready")
        up_full, h_ready = sem("up_full"), sem("h_ready")
        tv_ready, x_biased = sem("tv_ready"), sem("x_biased")
        first_max_full, first_max_free = sem("first_max_full"), sem("first_max_free")
        scores_ready, exp_done, lo_ready, product_done = (
            sem("scores_ready"), sem("exp_done"), sem("lo_ready"), sem("product_done"))
        lo_half_ready = sem("lo_half_ready")
        job_full, job_free = sem("job_full"), sem("job_free")
        u_free = sem("u_free")
        nm_ready, nm_rows_ready, nm_written = sem("nm_ready"), sem("nm_rows_ready"), sem("nm_written")
        dve_loop = sem("dve_loop")
        kq_ready = sem("kq_ready")
        k_hi_written = sem("k_hi_written")
        weights_ready = sem("weights_ready")
        stored = sem("stored")

        block = ctx.enter_context(nc.Block())

        def wait_emptied(engine, what, i):
            bank, use = bank_and_use(what, i)
            engine.wait_ge(gen_free[bank], use)

        def take(engine, what, i):
            bank, use = bank_and_use(what, i)
            engine.wait_ge(gen_full[bank], use)
            return gen_banks[bank]

        def free_of(what, i):
            return gen_free[bank_and_use(what, i)[0]]

        def wait_hi(engine, what, i):
            engine.wait_ge(hi_ready, HI_STEPS.index((what, i)) + 1)

        def tokens(b):
            return slice(QB * b, QB * (b + 1))

        def write_k_hi(sp, h):
            sp.dma_start(K1[h % 2][0:DK, :].bitcast(F32), KK[h % 2][0:DK, :].bitcast(F32)).then_inc(k_hi_written, 16)

        def write_maxima_rows(sp, g, count):
            sp.wait_ge(nm_rows_ready, count)
            ql = QL[g // NQB % 2]
            b = g % NQB
            sp.dma_start(ql[DK:DK + 2, QB * b:QB * (b + 1)].bitcast(F32), nm_rows[:, :]).then_inc(nm_written, 16)

        def n_of(at, g):
            return g if at.turn is None else g - 2 * NQB

        def head_of(at, h):
            return h if at.turn is None else at.turn * 2 + (h - 2)

        def stage_weights(head):
            own = bass.ds(head, 1)
            for twice in range(2):
                nc.vector.tensor_copy(Wh[:, :, twice, :],
                                      W4[:, own, :, :].bitcast(F32).rearrange("p o a d -> p (o a) d"))
            return nc.vector.tensor_copy(bh[:, :], bqk[:, own, :].rearrange("p o a -> p (o a)"))

        def split_k(h, b, full):
            own, kk = tokens(b), KK[h % 2]
            return nc.vector.scalar_tensor_tensor(kk[DK:P, own], full[DK:P, :], bh[DK:P, 1:2],
                                                  kk[DK:P, own].bitcast(F32), ALU.add, ALU.subtract)

        def split_q(h, b, full):
            own, qq, ql = tokens(b), QQ[h % 2], QL[h % 2]
            return nc.vector.scalar_tensor_tensor(ql[0:DK, own], full[0:DK, :], bh[0:DK, 0:1],
                                                  qq[0:DK, own].bitcast(F32), ALU.add, ALU.subtract)

        def split_kq(what, h, b, exact, link_):
            own = tokens(b)
            if what == "k":
                link_(nc.vector.tensor_copy(KK[h % 2][:, own], exact))
                return nc.vector.tensor_tensor(KK[h % 2][DK:P, own], exact[DK:P, :],
                                               KK[h % 2][DK:P, own].bitcast(F32), ALU.subtract)
            link_(nc.vector.tensor_copy(QQ[h % 2][:, own], exact))
            return nc.vector.tensor_tensor(QL[h % 2][0:DK, own], exact[0:DK, :],
                                           QQ[h % 2][0:DK, own].bitcast(F32), ALU.subtract)

        def negate_maxima(g, link_):
            link_(nc.vector.tensor_reduce(nmax[:, :], pm[:, g % 2, :, :], AXX, ALU.max, negate=True))
            link_(nc.vector.tensor_copy(nm_parts[:, 0, :].bitcast(F32R), nmax[:, :]))
            return nc.vector.tensor_tensor(nm_parts[:, 1, :].bitcast(F32R), nmax[:, :], nm_parts[:, 0, :],
                                           ALU.subtract)

        @block.sync
        def _(sp):
            z_view = z.rearrange("o (b t p) d -> b p (o t) d", p=P, t=TPB)
            for b in range(NQB):
                sp.dma_start(X[:, TPB * b:TPB * (b + 1), :], z_view[b]).then_inc(x_in[b], 16)
            for i, w in enumerate((wq, wk, wv)):
                for twice in range(2):
                    sp.dma_start(w_in[:, i, twice, :], w).then_inc(watt_in, 16)
            for rows, w in ((b_rows[:, 0, :], fcq_b), (b_rows[:, 1, :], fcq_b),
                            (b_rows[:, 2, :], fck_b), (b_rows[:, 3, :], fck_b)):
                sp.dma_start(rows, w.rearrange("(h d) -> h d", d=DK)).then_inc(wfc_in, 16)
            sp.dma_start(bv_rows[:, :], fcv_b.rearrange("(h d) -> h d", d=P)).then_inc(wfc_in, 16)
            sp.dma_start(bo_row[:, :], fco_b.rearrange("(o d) -> o d", o=1)).then_inc(wfc_in, 16)
            sp.dma_start(fv[:, :], fcv_w).then_inc(wfc_in, 16)
            sp.dma_start(fo[:, :, :], fco_w.rearrange("(c p) e -> p c e", p=P)).then_inc(wfc_in, 16)
            for f, w in ((fq, fcq_w), (fk, fck_w)):
                for half in range(2):
                    sp.dma_start(f[DK * half:DK * (half + 1), :, :].rearrange("p h d -> p (h d)"),
                                  w).then_inc(wfc_in, 16)
            sp.wait_ge(const_ready, 12)
            for b in range(NQB):
                wait_emptied(sp, "k", b)
            write_k_hi(sp, 0)
            def rows_of_block(g, turn):
                write_maxima_rows(sp, g, g + 1 if turn is None else turn * (2 * NQB) + (g + 1))
                h, b = divmod(g, NQB)
                if b == 2 and h + 1 < HEADS:
                    n = 2 * NQB * (h + 1) + NQB
                    sp.wait_ge(kq_ready, n if turn is None else turn * (2 * 2 * NQB) + n)
                    write_k_hi(sp, h + 1)

            rows_of_block(0, None)
            with sp.Fori(0, ROUNDS) as turn:
                for g in range(1, 1 + 2 * NQB):
                    rows_of_block(g, turn)
            for g in range(1 + ROUNDS * 2 * NQB, G_ALL):
                rows_of_block(g, None)
            out_view = out.rearrange("o (b t p) d -> b p (o t) d", p=P, t=TPB)
            for b in range(NQB):
                wait_emptied(sp, "D2", b)
                sp.dma_start(out_view[b], OUT[:, TPB * b:TPB * (b + 1), :]).then_inc(stored, 16)
            sp.wait_ge(stored, 16 * NQB)

        @block.gpsimd
        def _(pool):
            def fill(ins, n):
                ins.then_inc(const_ready, 1)
                pool.wait_ge(const_ready, n)

            fill(nc.gpsimd.memset(ident[:, :], 0.0), 1)
            fill(nc.gpsimd.affine_select(out=ident[:, :], in_=ident[:, :], compare_op=ALU.not_equal, fill=1.0,
                                         base=0, pattern=[[-1, P]], channel_multiplier=1), 2)
            fill(nc.gpsimd.memset(epsc[:, :], EPS), 3)
            fill(nc.gpsimd.memset(minus_half[:, :], -0.5), 4)
            links = [0]

            def rstd_of(b):
                own = slice(TPB * b, TPB * (b + 1))
                pool.wait_ge(stats_ready, links[0] + 1)
                links[0] += 1
                nc.gpsimd.tensor_tensor(var_eps[:, own], meanvar[:, own, 1], epsc[:, :], ALU.add
                                        ).then_inc(pool_chain, 1)
                pool.wait_ge(pool_chain, links[0])
                nc.gpsimd.tensor_tensor(rstd[:, own], var_eps[:, own], minus_half[:, :], ALU.pow
                                        ).then_inc(rstd_ready, 1)
                pool.wait_ge(rstd_ready, links[0])

            def constants(what, i):
                if (what, i) == ("stats0", 3):
                    fill(nc.gpsimd.memset(ones[:, :], 1.0), 5)
                    fill(nc.gpsimd.memset(ones16[:, :], 1.0), 6)
                for half, n, where in ((0, 7, ("stats1", 0)), (1, 10, ("stats1", 3))):
                    if (what, i) == where:
                        fill(nc.gpsimd.memset(QL[half][DK:P, :].bitcast(F32), 0.0), n)
                for half, n, where in ((0, 8, ("fc_parts", 1)), (1, 11, ("stats1", 3))):
                    if (what, i) == where:
                        fill(nc.gpsimd.memset(K1[half][DK:P, :].bitcast(F32), 0.0), n)
                        fill(nc.gpsimd.memset(K1[half][DK:DK + 2, :].bitcast(F32), 1.0), n + 1)

            for what, i in BEFORE:
                if what in ("stats0", "stats1"):
                    rstd_of(i)
                elif what == "in_parts":
                    pool.wait_ge(watt_in, 16 * 6)
                    wait_hi(pool, what, i)
                    nc.gpsimd.tensor_tensor(w_parts[:, 1, :, :], w_in[:, :, :, :].rearrange("p i a d -> p i (a d)"),
                                            w_parts[:, 0, :, :].bitcast(F32), ALU.subtract).then_inc(parts_ready, 1)
                    pool.wait_ge(parts_ready, 1)
                elif what == "fc_parts":
                    pool.wait_ge(wfc_in, 16 * 12)
                    wait_hi(pool, what, i)
                    nc.gpsimd.tensor_tensor(W4[:, :, 3 - 2 * i, :], (fk, fq)[i][:, :, :],
                                            W4[:, :, 2 - 2 * i, :].bitcast(F32), ALU.subtract).then_inc(fc_ready, 1)
                    pool.wait_ge(fc_ready, i + 1)
                constants(what, i)
            wait_emptied(pool, "bout", 0)
            pool.wait_ge(xn_ready, 2 * NQB)
            for t in range(TILES):
                nc.gpsimd.tensor_tensor(X[:, t, :], X[:, t, :], bout[:, :], ALU.add).then_inc(x_biased, 1)

            def step(at):
                t = at.absolute
                if t in LAST_RSTD:
                    rstd_of(LAST_RSTD[t])
                if not has_scores(t):
                    return
                pool.wait_ge(exp_done, at.t(1))
                if t >= RING:
                    pool.wait_ge(product_done, at.t(1 - RING))
                part = slice(0, QB if lo_shared(t) else KPS * QB)
                nc.gpsimd.tensor_tensor(Pl[:, t % RING, part], Pf[:, t % 2, part], Ph[:, t % RING, part],
                                        ALU.subtract).then_inc(lo_ready, 1)

            run_steps(nc.gpsimd, step)
            rstd_of(NQB - 1)

        @block.scalar
        def _(act):
            for i, w in enumerate((w_gate, w_up)):
                act.dma_start(w_int[:, i, :].rearrange("p (c d) -> p c d", c=HC),
                              w.rearrange("(c p) d -> p c d", p=P)).then_inc(wffn_in[i], 16)
            act.dma_start(w_int[:, 2, :], w_down).then_inc(wffn_in[2], 16)
            def hidden(k):
                act.wait_ge(gate_full, k + 1)
                if k >= 2:
                    act.wait_ge(h_ready, k - 1)
                nc.scalar.activation(sg[:, k % 2, :], gate_banks[k % 2], ACT.Silu, scale=SCALE
                                     ).then_inc(silu_ready, 1)

            def around(what, i):
                own = tokens(i)
                if what in ("H0", "H2"):
                    hidden(HIDDEN_STEPS.index((what, i)))
                elif what == "weights":
                    to = w_t[:, i, :] if i < 2 else w_down_t[:, :]
                    nc.scalar.copy(to, take(act, what, i)[:, 0:HIDDEN]).then_inc(free_of(what, i), 1)
                elif what in ("T0", "T1", "T2"):
                    nc.scalar.copy(XT[:, own], take(act, what, i)).then_inc(hi_ready, 1)
                elif what == "in_parts":
                    act.wait_ge(watt_in, 16 * 6)
                    nc.scalar.copy(w_parts[:, 0, :, :], w_in[:, :, :, :].rearrange("p i a d -> p i (a d)")
                                   ).then_inc(hi_ready, 1)
                elif what == "fc_parts":
                    act.wait_ge(wfc_in, 16 * 12)
                    if i == 0:
                        nc.scalar.copy(W4[:, :, 2, :], fk[:, :, :]).then_inc(hi_ready, 1)
                    else:
                        nc.scalar.activation(W4[:, :, 0, :], fq[:, :, :], ACT.Copy, scale=DK ** -0.5
                                             ).then_inc(fq_split, 1)
                        act.wait_ge(fq_split, 1)
                        nc.scalar.activation(fq[:, :, :], fq[:, :, :], ACT.Copy, scale=DK ** -0.5
                                             ).then_inc(hi_ready, 1)
                elif what in ("K", "Q"):
                    nc.scalar.copy((TK if what == "K" else TQ)[:, own], take(act, what, i)).then_inc(hi_ready, 1)
                elif what == "V":
                    nc.scalar.copy(TV[:, own], take(act, what, i)).then_inc(free_of(what, i), 1)
                elif what in ("k", "q"):
                    act.wait_ge(weights_ready, 1)
                    to, column = (KK, 1) if what == "k" else (QQ, 0)
                    nc.scalar.activation(to[0][:, own], take(act, what, i), ACT.Identity,
                                         bias=bh[:, column:column + 1]).then_inc(hi_ready, 1)
                elif what == "scale":
                    act.wait_ge(scale_ready, 1)
                    for b in range(NQB):
                        nc.scalar.activation(TV[:, tokens(b)], TV[:, tokens(b)], ACT.Copy, scale=ascale[:, :]
                                             ).then_inc(tv_ready, 1)
                elif what == "TT":
                    tiles = slice(TILES // 2 * i, TILES // 2 * (i + 1))
                    nc.scalar.copy(TT[:, tiles, 0, :], take(act, what, i).rearrange("p (t d) -> p t d", d=DK)
                                   ).then_inc(hi_ready, 1)
                elif what == "bout":
                    nc.scalar.copy(bout[:, :], take(act, what, i)[:, 0:EMBED]).then_inc(free_of(what, i), 1)
                elif what == "fcvT":
                    full = take(act, what, i).rearrange("p (c d) -> p c d", d=DK)
                    nc.scalar.copy(fvT[:, :, 0, :], full)
                    nc.scalar.copy(fvT[:, :, 1, :], full).then_inc(free_of(what, i), 1)
                elif what == "G":
                    to = GG[:, :].rearrange("p (a k r e) -> p a k r e", a=2, k=4, r=2)[:, i // 2, :, i % 2, :]
                    nc.scalar.activation(to, take(act, what, i).rearrange("p (k e) -> p k e", k=4), ACT.Copy,
                                         scale=aback[:, :]).then_inc(free_of(what, i), 1)
                elif what == "scores":
                    step(Turn(i, None, i))

            def step(at):
                t = at.absolute
                if not has_scores(t):
                    return
                act.wait_ge(scores_ready, at.t(1))
                if t >= RING:
                    act.wait_ge(product_done, at.t(1 - RING))
                scores = S[t % 2]
                nc.scalar.activation(Ph[:, t % RING, :].rearrange("p (k q) -> p k q", k=KPS), scores, ACT.Exp)
                if t >= 2:
                    act.wait_ge(lo_ready, at.t(-1))
                    if lo_shared(t - 2):
                        act.wait_ge(lo_half_ready, lo_halves(t - 2))
                nc.scalar.activation(Pf[:, t % 2, :].rearrange("p (k q) -> p k q", k=KPS), scores,
                                     ACT.Exp).then_inc(exp_done, 1)

            def step_and_products(at):
                if at.absolute >= EARLY:
                    step(at)
                t = at.absolute
                if t % SPB == LAG - 1 and SPB <= t < STEPS + SPB:
                    act.wait_ge(product_done, at.t(1 - LAG))
                    nc.scalar.copy(U, UB)
                    nc.scalar.copy(sums, SUMB).then_inc(u_free, 1)
                if t == STEPS:
                    nc.scalar.activation(warm[:, :], ident[:, 0:1], ACT.Silu)
                for what, i in AFTER_STEP.get(t, []):
                    around(what, i)

            act.wait_ge(const_ready, 2)
            nc.scalar.activation(warm[:, :], ident[:, 0:1], ACT.Silu)
            for what, i in BEFORE:
                around(what, i)
            run_steps(nc.scalar, step_and_products)
            for what, i in AFTER_ALL:
                around(what, i)

        @block.vector
        def _(dve):
            chained = [0]

            def link(ins):
                chained[0] += 1
                ins.then_inc(dve_chain, 1)
                dve.wait_ge(dve_chain, chained[0])

            norms = [0]

            def stats_of(b):
                for t in range(TPB * b, TPB * (b + 1)):
                    last = nc.vector.bn_stats(stats[:, t, :], X[:, t, :])
                link(last)
                for t in range(TPB * b, TPB * (b + 1)):
                    last = nc.vector.bn_aggr(meanvar[:, t, :], stats[:, t, :])
                last.then_inc(stats_ready, 1)

            def normalise(what, b):
                n = NORMS.index((what, b)) + 1
                dve.wait_ge(stats_ready, n)
                dve.wait_ge(rstd_ready, n)
                for t in range(TPB * b, TPB * (b + 1)):
                    ins = nc.vector.tensor_scalar(XN[:, t, :], X[:, t, :], meanvar[:, t, 0:1], rstd[:, t:t + 1],
                                                  ALU.subtract, ALU.mult)
                ins.then_inc(xn_ready, 1)

            def hidden(k, b, c):
                if k == HIDDEN_STEPS.index(("H2", 0)):
                    dve.wait_ge(lo_ready, STEPS - 1)
                if k == HIDDEN_STEPS.index(("H2", 2)):
                    dve.wait_ge(lo_ready, STEPS)
                dve.wait_ge(up_full, k + 1)
                dve.wait_ge(silu_ready, k + 1)
                nc.vector.tensor_tensor(hT[:, b % 2, c, :], up_banks[k % 2], sg[:, k % 2, :],
                                        ALU.mult).then_inc(h_ready, 1)

            def around(what, i):
                own = tokens(i)
                tiles = slice(TPB * i, TPB * (i + 1))
                if what in ("stats0", "stats1"):
                    if what == "stats0":
                        dve.wait_ge(x_in[i], 16)
                    else:
                        wait_emptied(dve, "D0", i)
                    stats_of(i)
                elif what == "weights":
                    dve.wait_ge(wffn_in[i], 16)
                    nc.vector.tensor_copy(w_f[:, i, :], w_int[:, i, :]).then_inc(deq_ready, 1)
                elif what == "stats2":
                    dve.wait_ge(job_free, jobs.n)
                    stats_of(i)
                elif what in ("norm0", "norm1", "norm2"):
                    normalise(what, i)
                elif what == "biases":
                    full = take(dve, what, i)
                    nc.vector.tensor_scalar(bqk[:, :, 0], full[:, 0:HEADS], DK ** -0.5, None, ALU.mult)
                    nc.vector.tensor_copy(bqk[:, :, 1], full[:, HEADS:2 * HEADS])
                    nc.vector.tensor_copy(bv[:, :], full[:, 2 * HEADS:2 * HEADS + HEADS // 2]
                                          ).then_inc(free_of(what, i), 1)
                elif what in ("T0", "T1", "T2"):
                    full = take(dve, what, i)
                    wait_hi(dve, what, i)
                    nc.vector.tensor_tensor(XTL[:, own], full, XT[:, own].bitcast(F32), ALU.subtract
                                            ).then_inc(free_of(what, i), 1)
                elif what in ("H0", "H2"):
                    hidden(HIDDEN_STEPS.index((what, i)), *divmod(i, HC))
                elif what in ("D0", "D2"):
                    full = take(dve, what, i).rearrange("p (t d) -> p t d", t=TPB)
                    to = X if what == "D0" else OUT
                    nc.vector.scalar_tensor_tensor(to[:, tiles, :], full, 0.5 * SCALE * SCALE, X[:, tiles, :],
                                                   ALU.mult, ALU.add).then_inc(free_of(what, i), 1)
                elif what == "stage":
                    wait_emptied(dve, "biases", 0)
                    dve.wait_ge(fc_ready, 2)
                    stage_weights(0).then_inc(weights_ready, 1)
                elif what in ("K", "Q"):
                    T = TK if what == "K" else TQ
                    full = take(dve, what, i)
                    wait_hi(dve, what, i)
                    nc.vector.tensor_tensor(T[DK:P, own], full[DK:P, :], T[DK:P, own].bitcast(F32),
                                            ALU.subtract).then_inc(free_of(what, i), 1)
                elif what in ("k", "q"):
                    full = take(dve, what, i)
                    dve.wait_ge(weights_ready, 1)
                    wait_hi(dve, what, i)
                    (split_k if what == "k" else split_q)(0, i, full).then_inc(free_of(what, i), 1)
                elif what == "M0":
                    dve.wait_ge(first_max_full, i + 1)
                    nc.vector.reduce_max(pm[:, 0, i // 2, 2 * (i % 2):2 * (i % 2) + 2], S[i % 2], AXX
                                         ).then_inc(first_max_free, 1)
                elif what == "M1":
                    nc.vector.reduce_max(pm[:, 1, i // 4, i % 4:i % 4 + 1], take(dve, what, i), AXX
                                         ).then_inc(free_of(what, i), 1)
                elif what == "nm":
                    dve.wait_ge(first_max_free, 2 * TPB)
                    negate_maxima(0, link).then_inc(nm_ready, 1)
                    nc.vector.tensor_copy(nm_rows[:, :], take(dve, what, i)[0:2 * TPB, 0:P]
                                          ).then_inc(nm_rows_ready, 1)
                    dve.wait_ge(nm_rows_ready, 1)
                    nc.vector.tensor_copy(signal[:, :], epsc[:, 0:1]).then_inc(free_of(what, i), 1)
                elif what == "V":
                    wait_emptied(dve, "V", i)
                    ins = nc.vector.tensor_reduce(amax_by[:, i:i + 1], TV[:, own], AXX, ALU.max,
                                                  apply_absolute_value=True)
                    if i == NQB - 1:
                        link(ins)
                elif what == "scale":
                    link(nc.vector.reduce_max(amax[:, :], amax_by[:, :], AXX))
                    link(nc.vector.tensor_scalar(asafe[:, :], amax[:, :], 1e-30, None, ALU.max))
                    link(nc.vector.reciprocal(arec[:, :], asafe[:, :]))
                    nc.vector.tensor_scalar(aback[:, :], asafe[:, :], 1.0 / T_RANGE, None, ALU.mult)
                    nc.vector.tensor_scalar(ascale[:, :], arec[:, :], T_RANGE, None, ALU.mult
                                            ).then_inc(scale_ready, 1)
                elif what == "TT":
                    full = take(dve, what, i).rearrange("p (t d) -> p t d", d=DK)
                    half = slice(TILES // 2 * i, TILES // 2 * (i + 1))
                    wait_hi(dve, what, i)
                    nc.vector.tensor_tensor(TT[:, half, 1, :], full, TT[:, half, 0, :], ALU.subtract
                                            ).then_inc(free_of(what, i), 1)

            for what, i in BEFORE:
                around(what, i)
            for bank, uses in enumerate(last_uses(BEFORE)):
                dve.wait_ge(gen_free[bank], uses)
            nc.vector.tensor_copy(signal[:, :], epsc[:, 0:1]).then_inc(kq_ready, 2 * NQB)

            jobs = Count(JOBS_PER_PAIR)
            chain = Count(CHAIN_PER_PAIR)
            sums_job = [0]

            def step(at):
                t = at.absolute
                g, j = divmod(t, SPB)
                b = g % NQB

                def loop_link(ins):
                    chain.add(at)
                    ins.then_inc(dve_loop, 1)
                    dve.wait_ge(dve_loop, chain.value(at))

                def take_job():
                    jobs.add(at)
                    dve.wait_ge(job_full, jobs.value(at))
                    return JOB_BANKS[(jobs.n - 1) % 2]

                def reduce_maxima(i):
                    chunk = 2 * (j % 2) + i
                    nc.vector.reduce_max(pm[:, g % 2, j // 2, chunk:chunk + 1], take_job(), AXX
                                         ).then_inc(job_free, 1)

                if lo_shared(t):
                    dve.wait_ge(exp_done, t + 1)
                    dve.wait_ge(product_done, t + 1 - RING)
                    half = slice(QB, KPS * QB)
                    nc.vector.tensor_tensor(Pl[:, t % RING, half], Pf[:, t % 2, half], Ph[:, t % RING, half],
                                            ALU.subtract).then_inc(lo_half_ready, 1)
                if j == 0 and g + 1 < G_ALL:
                    if g >= 1:
                        dve.wait_ge(job_free, jobs.value(at))
                    negate_maxima(g + 1, loop_link).then_inc(nm_ready, 1)
                projected = None
                if has_maxima(t):
                    reduce_maxima(0)
                for job, n, i in side_jobs(t):
                    SIDE = take_job()
                    if job == "maxima":
                        dve.wait_ge(nm_written, at.value(16 * n_of(at, n), 16 * 2 * NQB))
                        nc.vector.tensor_copy(nm_rows[:, :], SIDE[0:2 * TPB, 0:P]).then_inc(nm_rows_ready, 1)
                        dve.wait_ge(nm_rows_ready, at.value(n_of(at, n) + 1, 2 * NQB))
                        nc.vector.tensor_copy(signal[:, :], epsc[:, 0:1]).then_inc(job_free, 1)
                    elif job in "kq":
                        exact = sg[:, i % 2, :]
                        bias = bh[:, 1:2] if job == "k" else bh[:, 0:1]
                        nc.vector.tensor_scalar(exact, SIDE, bias, None, ALU.add).then_inc(job_free, 1)
                        projected = (job, n, i, exact, jobs.n)
                    elif job == "sums":
                        loop_link(nc.vector.reduce_sum(qsum[:, :], SIDE.rearrange(
                            "p (t i o) -> p t i o", t=TPB, o=32)[:, :, :, 0], AXX))
                        nc.vector.reciprocal(rsum[:, :], qsum[:, :]).then_inc(job_free, 1)
                        sums_job[0] = jobs.n
                    else:
                        dve.wait_ge(job_free, jobs.value(at, sums_job[0]))
                        if g == 1:
                            dve.wait_ge(x_biased, TILES)
                        for q in range(TPB):
                            tile = TPB * (n % NQB) + q
                            ins = nc.vector.scalar_tensor_tensor(X[:, tile, :], SIDE[:, P * q:P * (q + 1)],
                                                                 rsum[:, q:q + 1], X[:, tile, :], ALU.mult, ALU.add)
                        ins.then_inc(job_free, 1)
                if has_maxima(t):
                    reduce_maxima(1)
                if projected:
                    what, n, i, exact, job = projected
                    dve.wait_ge(job_free, jobs.value(at, job))
                    split_kq(what, n, i, exact, loop_link).then_inc(kq_ready, 1)
                if b == 3 and j == SPB - 1 and g // NQB + 2 < HEADS:
                    stage_weights(head_of(at, g // NQB + 2)).then_inc(weights_ready, 1)
                if t in LAST_STATS:
                    dve.wait_ge(job_free, jobs.n)
                    stats_of(LAST_STATS[t])
                if t in LAST_NORM:
                    normalise("norm2", LAST_NORM[t])
                for what, i in AFTER_STEP.get(t, []):
                    around(what, i)

            stage_weights(1).then_inc(weights_ready, 1)
            run_steps(nc.vector, step)
            for what, i in AFTER_ALL:
                around(what, i)

        @block.tensor
        def _(pe):
            def give(what, i):
                bank, use = bank_and_use(what, i)
                if use > 1:
                    pe.wait_ge(gen_free[bank], use - 1)
                return gen_banks[bank]

            def transpose(to, of):
                k, m = of.shape
                return nc.tensor.transpose(to, of, ident[0:k, 0:k])

            def project(full, parts, T, b):
                for i in range(2):
                    last = nc.tensor.matmul(full, Wh[:, parts + i, :, :].rearrange("p a d -> p (a d)"),
                                            T[:, tokens(b)], start=i == 0, stop=i == 1)
                return last

            def hidden(k, b, c):
                if k >= 2:
                    pe.wait_ge(h_ready, k - 1)
                for full, w, done in ((gate_banks, 0, gate_full), (up_banks, 1, up_full)):
                    for part, x in enumerate((XT, XTL)):
                        last = nc.tensor.matmul(full[k % 2], w_t[:, w, P * c:P * (c + 1)], x[:, tokens(b)],
                                                start=part == 0, stop=part == 1)
                    last.then_inc(done, 1)

            def around(what, i):
                own = tokens(i)
                if what in ("H0", "H2"):
                    if (what, i) == HIDDEN_STEPS[0]:
                        for w in range(2):
                            wait_emptied(pe, "weights", w)
                    wait_emptied(pe, "T" + what[1], i // HC)
                    hidden(HIDDEN_STEPS.index((what, i)), *divmod(i, HC))
                    return
                if what == "M0":
                    tile, half = divmod(i, 2)
                    if i == 0:
                        for b in range(NQB):
                            wait_emptied(pe, "k", b)
                        wait_emptied(pe, "q", 0)
                        pe.wait_ge(h_ready, NQB * HC)
                    if i >= 2:
                        pe.wait_ge(first_max_free, i - 1)
                    for c in range(2):
                        last = nc.tensor.matmul(S[i % 2][:, c, :], QQ[0][:, P * tile:P * (tile + 1)],
                                                KK[0][:, tokens(2 * half + c)], start=True, stop=True)
                    last.then_inc(first_max_full, 1)
                    return
                if what == "scores":
                    pe.wait_ge(first_max_free, 2 * TPB)
                    scores(Turn(i, None, i))
                    return
                if what in NO_BANK:
                    return
                full = give(what, i)
                if what == "weights":
                    pe.wait_ge(deq_ready, i + 1)
                    for c in range(HC):
                        last = transpose(full[:, P * c:P * (c + 1)], w_f[:, i, P * c:P * (c + 1)])
                elif what in ("T0", "T1", "T2"):
                    pe.wait_ge(xn_ready, NORMS.index(("norm" + what[1], i)) + 1)
                    for k in range(TPB):
                        last = transpose(full[:, P * k:P * (k + 1)], XN[:, TPB * i + k, :])
                elif what in ("D0", "D2"):
                    if (what, i) == ("D0", 0):
                        wait_emptied(pe, "weights", 2)
                    pe.wait_ge(h_ready, HIDDEN_STEPS.index(("H" + what[1], HC * i + HC - 1)) + 1)
                    for k in range(TPB):
                        for c in range(HC):
                            last = nc.tensor.matmul(full[:, P * k:P * (k + 1)], hT[:, i % 2, c, P * k:P * (k + 1)],
                                                    w_down_t[:, P * c:P * (c + 1)], start=c == 0, stop=c == HC - 1)
                elif what == "biases":
                    pe.wait_ge(wfc_in, 16 * 12)
                    transpose(full[:, 0:HEADS], b_rows[:, 0:2, :].rearrange("p a d -> p (a d)"))
                    transpose(full[:, HEADS:2 * HEADS], b_rows[:, 2:4, :].rearrange("p a d -> p (a d)"))
                    last = transpose(full[:, 2 * HEADS:2 * HEADS + HEADS // 2], bv_rows[:, :])
                elif what == "fcvT":
                    for c in range(HEADS // 2):
                        last = transpose(full[:, DK * c:DK * (c + 1)], fv[:, P * c:P * (c + 1)])
                elif what in ("K", "Q", "V"):
                    wait_emptied(pe, "T1", i)
                    pe.wait_ge(parts_ready, 1)
                    w = "QKV".index(what)
                    for n, (part, x) in enumerate(((0, XT), (0, XTL), (1, XT))):
                        last = nc.tensor.matmul(full, w_parts[:, part, w, :], x[:, own], start=n == 0, stop=n == 2)
                elif what in ("k", "q"):
                    pe.wait_ge(weights_ready, 1)
                    wait_emptied(pe, what.upper(), i)
                    last = project(full, 2 if what == "k" else 0, TK if what == "k" else TQ, i)
                elif what == "M1":
                    if i == 0:
                        wait_emptied(pe, "q", 1)
                    tile = TPB + i // 4
                    last = nc.tensor.matmul(full, QQ[0][:, P * tile:P * (tile + 1)], KK[0][:, tokens(i % 4)],
                                            start=True, stop=True)
                elif what == "nm":
                    pe.wait_ge(nm_ready, 1)
                    last = transpose(full[0:2 * TPB, 0:P], nm_parts[:, :, :].rearrange("p a t -> p (a t)"))
                elif what == "TT":
                    pe.wait_ge(tv_ready, NQB)
                    for t in range(TILES // 2):
                        tile = TILES // 2 * i + t
                        last = transpose(full[:, DK * t:DK * (t + 1)], TV[0:DK, P * tile:P * (tile + 1)])
                elif what == "bout":
                    wait_emptied(pe, "biases", 0)
                    pe.wait_ge(const_ready, 12)
                    for c in range(HEADS // 2):
                        nc.tensor.matmul(full[:, 0:EMBED], bv[:, c:c + 1].to_broadcast([P, P]), fo[:, c, :],
                                         start=c == 0, stop=False)
                    last = nc.tensor.matmul(full[:, 0:EMBED], ones[0:1, :], bo_row[:, :], start=False, stop=True)
                elif what == "G":
                    wait_emptied(pe, "fcvT", 0)
                    for k in range(4):
                        h = 8 * (i // 2) + 2 * k + i % 2
                        rows = slice(DK * (h % 2), DK * (h % 2 + 1))
                        last = nc.tensor.matmul(full[:, P * k:P * (k + 1)],
                                                fvT[rows, h // 2, :, :].rearrange("p a d -> p (a d)"),
                                                fo[rows, h // 2, :], start=True, stop=True)
                last.then_inc(gen_full[bank_and_use(what, i)[0]], 1)

            def scores(at):
                t = at.absolute
                g, j = divmod(t, SPB)
                b, h = g % NQB, g // NQB
                if j == 0 and b == 0:
                    pe.wait_ge(k_hi_written, at.value(16 * (h + 1 - (0 if at.turn is None else 2)), 16 * 2))
                if j == 0:
                    pe.wait_ge(nm_written, at.value(16 * (n_of(at, g) + 1), 16 * 2 * NQB))
                if t >= 2:
                    pe.wait_ge(exp_done, at.t(-1))
                for k in range(KPS):
                    tile = KPS * j + k
                    keys = slice(P * tile, P * (tile + 1))
                    nc.tensor.matmul(S[t % 2][:, k, :], KK[h % 2][:, keys], QQ[h % 2][:, tokens(b)],
                                     start=True, stop=False)
                    last = nc.tensor.matmul(S[t % 2][:, k, :], K1[h % 2][:, keys], QL[h % 2][:, tokens(b)],
                                            start=False, stop=True)
                last.then_inc(scores_ready, 1)

            pe.wait_ge(const_ready, 2)
            for _ in range(WARMING):
                nc.tensor.matmul(gate_banks[0][:, 0:P], ident[:, :], ident[:, :], start=True, stop=True)
            for what, i in BEFORE:
                around(what, i)
            for bank, uses in enumerate(last_uses(BEFORE)):
                pe.wait_ge(gen_free[bank], uses)

            jobs = Count(JOBS_PER_PAIR)

            def give_job(at):
                if jobs.n >= 2:
                    pe.wait_ge(job_free, at.value(jobs.count(at) - 1, JOBS_PER_PAIR))
                jobs.add(at)
                return JOB_BANKS[(jobs.n - 1) % 2]

            def maxima(at, i):
                t = at.absolute
                g, j = divmod(t, SPB)
                gm = g + AHEAD
                hm, bm = divmod(gm, NQB)
                if j == 0 and i == 0:
                    head = hm if at.turn is None else hm - 2
                    pe.wait_ge(kq_ready, at.value(2 * NQB * head + NQB + bm + 1, 2 * 2 * NQB))
                tile = TPB * bm + j // 2
                keys = QB * (2 * (j % 2) + i)
                nc.tensor.matmul(give_job(at), QQ[hm % 2][:, P * tile:P * (tile + 1)], KK[hm % 2][:, keys:keys + QB],
                                 start=True, stop=True).then_inc(job_full, 1)

            def products_hi(at):
                s = at.absolute - LAG
                js = s % SPB
                pe.wait_ge(lo_ready, at.t(1 - LAG))
                if lo_shared(s):
                    pe.wait_ge(lo_half_ready, lo_halves(s))
                if js == 0 and s >= SPB:
                    pe.wait_ge(u_free, at.value(n_of(at, s // SPB), 2 * NQB))
                for k in range(KPS):
                    tile = KPS * js + k
                    nc.tensor.matmul(UB, TT[:, tile, :, :].rearrange("p a d -> p (a d)"),
                                     Ph[:, s % RING, QB * k:QB * (k + 1)], start=js == 0 and k == 0, stop=False,
                                     skip_group_check=True)

            def products_lo(at):
                s = at.absolute - LAG
                js = s % SPB
                for k in range(KPS):
                    tile = KPS * js + k
                    nc.tensor.matmul(UB[DK * k:DK * (k + 1), :], TT[:, tile, 0, :],
                                     Pl[:, s % RING, QB * k:QB * (k + 1)], start=False, stop=js == SPB - 1,
                                     skip_group_check=True)
                for i in range(4):
                    part = (Ph, Pl)[i // 2]
                    last = nc.tensor.matmul(SUMB[32 * i:32 * (i + 1), :], ones16[:, :],
                                            part[:, s % RING, QB * (i % 2):QB * (i % 2 + 1)],
                                            start=js == 0, stop=js == SPB - 1)
                last.then_inc(product_done, 1)

            def step(at):
                t = at.absolute
                g, j = divmod(t, SPB)
                if has_scores(t) and t >= EARLY:
                    scores(at)
                if has_maxima(t):
                    maxima(at, 0)
                if has_product(t):
                    products_hi(at)
                for job, n, i in side_jobs(t):
                    if t == STEPS + LAG:
                        for b in range(2):
                            wait_emptied(pe, "T2", b)
                    SIDE = give_job(at)
                    if job == "maxima":
                        pe.wait_ge(nm_ready, at.value(n_of(at, n) + 1, 2 * NQB))
                        last = transpose(SIDE[0:2 * TPB, 0:P], nm_parts[:, :, :].rearrange("p a t -> p (a t)"))
                    elif job in "kq":
                        if job == "k" and i == 0:
                            pe.wait_ge(weights_ready, at.value(n + 1 - (0 if at.turn is None else 2), 2))
                        last = project(SIDE, 2 if job == "k" else 0, TK if job == "k" else TQ, i)
                    elif job == "sums":
                        pe.wait_ge(u_free, at.value(n_of(at, n) + 1, 2 * NQB))
                        for q in range(TPB):
                            last = transpose(SIDE[:, P * q:P * q + SUM_ROWS], sums[0:SUM_ROWS, P * q:P * (q + 1)])
                    else:
                        head = head_of(at, n // NQB)
                        for q in range(TPB):
                            last = nc.tensor.matmul(SIDE[:, P * q:P * (q + 1)], U[:, P * q:P * (q + 1)],
                                                    GG[:, bass.ds(head * EMBED, EMBED)], start=True, stop=True)
                    last.then_inc(job_full, 1)
                if has_product(t):
                    products_lo(at)
                if has_maxima(t):
                    maxima(at, 1)
                if t == STEPS:
                    pe.wait_ge(job_free, jobs.n)
                    pe.wait_ge(exp_done, STEPS)
                for what, i in AFTER_STEP.get(t, []):
                    around(what, i)

            run_steps(nc.tensor, step)
            pe.wait_ge(job_free, jobs.n)
            for what, i in AFTER_ALL:
                around(what, i)


_INPUTS = ("z", "wq", "wk", "wv", "fcq_w", "fcq_b", "fck_w", "fck_b", "fcv_w", "fcv_b", "fco_w", "fco_b")
_FFN = ("w_gate", "w_up", "w_down")


def kernel(**inputs):
    import numpy as np
    import concourse.bacc as bacc
    from concourse.bass_utils import run_bass_kernel_spmd

    nc = bacc.Bacc("TRN2", target_bir_lowering=False, num_devices=1)
    arrays, args = {}, {}
    for name in _INPUTS + _FFN:
        a = np.ascontiguousarray(inputs[("L0_attn_" if name in _INPUTS else "L0_ffn_") + name])
        arrays[f"in_{name}"] = a
        args[name] = nc.dram_tensor(f"in_{name}", a.shape, mybir.dt.from_np(a.dtype), kind="ExternalInput").ap()
    args["out"] = nc.dram_tensor("out", (1, SEQ, EMBED), F32, kind="ExternalOutput").ap()
    build(nc, **args)
    result = run_bass_kernel_spmd(nc, [arrays], core_ids=[0])
    return result.results[0]["out"]
```
